# Optimizing a Trainium2 kernel written in Bass

```python
import numpy as np
import jax
import jax.numpy as jnp

def _softmax(x, axis=-1):
    return jax.nn.softmax(x, axis=axis)

def _gelu(x):
    return jax.nn.gelu(x, approximate=True)

def _silu(x):
    return jax.nn.silu(x)

def _sigmoid(x):
    return jax.nn.sigmoid(x)

def _layernorm(x, axis=-1, eps=1e-05):
    m = jnp.mean(x, axis=axis, keepdims=True)
    v = jnp.var(x, axis=axis, keepdims=True)
    return (x - m) / jnp.sqrt(v + eps)

def _scatter_add(tgt, idx, src, axis=0):
    return tgt.at[idx].add(src)

def _segment_sum(src, seg, n):
    return jax.ops.segment_sum(src, seg, n)
kernel_name = 'mk_conv_seq_d1_conv_nchw128_r4_c9ecd3'

def setup_inputs(seed: int=0):
    np.random.seed(seed)
    _w = jnp.asarray

    def _rec_inputs():
        import jax
        import jax.numpy as jnp
        _gk = jax.random.key(seed)
        x = -0.000125 + 0.9999 * jax.random.normal(jax.random.fold_in(_gk, 1), (4, 32, 64, 64), jnp.float32)
        return x
    x = _rec_inputs()

    def _L0_conv_setup():
        import jax, jax.numpy as jnp
        import numpy as np
        WS = 8
        NH = 4

        def _rel_pos_index(ws):
            coords = np.stack(np.meshgrid(np.arange(ws), np.arange(ws), indexing='ij'))
            flat = coords.reshape(2, -1)
            rel = flat[:, :, None] - flat[:, None, :]
            rel = rel.transpose(1, 2, 0).astype(np.int64)
            rel[:, :, 0] += ws - 1
            rel[:, :, 1] += ws - 1
            rel[:, :, 0] *= 2 * ws - 1
            return rel.sum(-1)
        _RPI = jnp.asarray(_rel_pos_index(WS))

        def _ln(t, g, b, eps=1e-05):
            mu = jnp.mean(t, axis=-1, keepdims=True)
            var = jnp.mean(jnp.square(t - mu), axis=-1, keepdims=True)
            return (t - mu) * jax.lax.rsqrt(var + eps) * g + b
        key = jax.random.key(seed)
        ks = jax.random.split(key, 8)
        C = 32
        inp = {'x': jax.random.normal(ks[0], (4, C, 64, 64), jnp.float32), 'ln1_g': jnp.ones((C,), jnp.float32), 'ln1_b': jnp.zeros((C,), jnp.float32), 'qkv_w': jax.random.normal(ks[1], (3 * C, C), jnp.float32) * 0.02, 'qkv_b': jnp.zeros((3 * C,), jnp.float32), 'rpb': jax.random.normal(ks[2], ((2 * WS - 1) ** 2, NH), jnp.float32) * 0.02, 'proj_w': jax.random.normal(ks[3], (C, C), jnp.float32) * 0.02, 'proj_b': jnp.zeros((C,), jnp.float32), 'ln2_g': jnp.ones((C,), jnp.float32), 'ln2_b': jnp.zeros((C,), jnp.float32), 'fc1_w': jax.random.normal(ks[4], (4 * C, C), jnp.float32) * 0.02, 'fc1_b': jnp.zeros((4 * C,), jnp.float32), 'fc2_w': jax.random.normal(ks[5], (C, 4 * C), jnp.float32) * 0.02, 'fc2_b': jnp.zeros((C,), jnp.float32)}
        return inp
    _L0_conv_all = _L0_conv_setup()
    _L0_conv_in = {k: v for k, v in _L0_conv_all.items() if k in ('ln1_g', 'ln1_b', 'qkv_w', 'qkv_b', 'rpb', 'proj_w', 'proj_b', 'ln2_g', 'ln2_b', 'fc1_w', 'fc1_b', 'fc2_w', 'fc2_b')}
    del _L0_conv_all
    return {'x': x, 'L0_conv_ln1_g': _L0_conv_in['ln1_g'], 'L0_conv_ln1_b': _L0_conv_in['ln1_b'], 'L0_conv_qkv_w': _L0_conv_in['qkv_w'], 'L0_conv_qkv_b': _L0_conv_in['qkv_b'], 'L0_conv_rpb': _L0_conv_in['rpb'], 'L0_conv_proj_w': _L0_conv_in['proj_w'], 'L0_conv_proj_b': _L0_conv_in['proj_b'], 'L0_conv_ln2_g': _L0_conv_in['ln2_g'], 'L0_conv_ln2_b': _L0_conv_in['ln2_b'], 'L0_conv_fc1_w': _L0_conv_in['fc1_w'], 'L0_conv_fc1_b': _L0_conv_in['fc1_b'], 'L0_conv_fc2_w': _L0_conv_in['fc2_w'], 'L0_conv_fc2_b': _L0_conv_in['fc2_b']}

def reference(x, L0_conv_ln1_g, L0_conv_ln1_b, L0_conv_qkv_w, L0_conv_qkv_b, L0_conv_rpb, L0_conv_proj_w, L0_conv_proj_b, L0_conv_ln2_g, L0_conv_ln2_b, L0_conv_fc1_w, L0_conv_fc1_b, L0_conv_fc2_w, L0_conv_fc2_b):
    import jax
    import jax.numpy as jnp

    def _L0_conv_ref(x, ln1_g, ln1_b, qkv_w, qkv_b, rpb, proj_w, proj_b, ln2_g, ln2_b, fc1_w, fc1_b, fc2_w, fc2_b):
        import jax, jax.numpy as jnp
        import numpy as np
        WS = 8
        NH = 4

        def _rel_pos_index(ws):
            coords = np.stack(np.meshgrid(np.arange(ws), np.arange(ws), indexing='ij'))
            flat = coords.reshape(2, -1)
            rel = flat[:, :, None] - flat[:, None, :]
            rel = rel.transpose(1, 2, 0).astype(np.int64)
            rel[:, :, 0] += ws - 1
            rel[:, :, 1] += ws - 1
            rel[:, :, 0] *= 2 * ws - 1
            return rel.sum(-1)
        _RPI = jnp.asarray(_rel_pos_index(WS))

        def _ln(t, g, b, eps=1e-05):
            mu = jnp.mean(t, axis=-1, keepdims=True)
            var = jnp.mean(jnp.square(t - mu), axis=-1, keepdims=True)
            return (t - mu) * jax.lax.rsqrt(var + eps) * g + b
        B, C, H, W = x.shape
        ws, nH = (WS, NH)
        N = ws * ws
        hd = C // nH
        xw = x.reshape(B, C, H // ws, ws, W // ws, ws)
        xw = xw.transpose(0, 2, 4, 3, 5, 1).reshape(-1, N, C)
        h = _ln(xw, ln1_g, ln1_b)
        qkv = h @ qkv_w.T + qkv_b
        qkv = qkv.reshape(-1, N, 3, nH, hd).transpose(2, 0, 3, 1, 4)
        q, k, v = (qkv[0], qkv[1], qkv[2])
        attn = jnp.einsum('whnd,whmd->whnm', q * hd ** (-0.5), k)
        bias = rpb[_RPI.reshape(-1)].reshape(N, N, nH).transpose(2, 0, 1)
        attn = jax.nn.softmax(attn + bias[None], axis=-1)
        o = jnp.einsum('whnm,whmd->whnd', attn, v)
        o = o.transpose(0, 2, 1, 3).reshape(-1, N, C)
        o = o @ proj_w.T + proj_b
        xw = xw + o
        h = _ln(xw, ln2_g, ln2_b)
        h = jax.nn.gelu(h @ fc1_w.T + fc1_b, approximate=False)
        h = h @ fc2_w.T + fc2_b
        xw = xw + h
        xw = xw.reshape(B, H // ws, W // ws, ws, ws, C)
        out = xw.transpose(0, 5, 1, 3, 2, 4).reshape(B, C, H, W)
        return out

    def _gn(v, G=32, eps=1e-05):
        B_, C_, H_, W_ = v.shape
        g = v.reshape(B_, G, C_ // G, H_, W_)
        m = jnp.mean(g, axis=(2, 3, 4), keepdims=True)
        s = jnp.var(g, axis=(2, 3, 4), keepdims=True)
        return ((g - m) / jnp.sqrt(s + eps)).reshape(v.shape)

    def _ln_c(v, eps=1e-06):
        m = jnp.mean(v, axis=1, keepdims=True)
        s = jnp.var(v, axis=1, keepdims=True)
        return (v - m) / jnp.sqrt(s + eps)

    def _ln_t(v, eps=1e-05):
        m = jnp.mean(v, axis=-1, keepdims=True)
        s = jnp.var(v, axis=-1, keepdims=True)
        return (v - m) / jnp.sqrt(s + eps)

    def _to_tokens(v):
        B_, C_, H_, W_ = v.shape
        return v.reshape(B_, C_, H_ * W_).transpose(0, 2, 1)

    def _from_tokens(t, like):
        B_, C_, H_, W_ = like.shape
        return t.transpose(0, 2, 1).reshape(B_, C_, H_, W_)
    x = _L0_conv_ref(x, L0_conv_ln1_g, L0_conv_ln1_b, L0_conv_qkv_w, L0_conv_qkv_b, L0_conv_rpb, L0_conv_proj_w, L0_conv_proj_b, L0_conv_ln2_g, L0_conv_ln2_b, L0_conv_fc1_w, L0_conv_fc1_b, L0_conv_fc2_w, L0_conv_fc2_b)
    return x

_drawn_inputs = setup_inputs


def setup_inputs(seed=0):
    import zlib

    import numpy as np

    out = dict(_drawn_inputs(seed))
    spreads = {'L0_conv_ln1_g': (1.0, 0.6),
     'L0_conv_ln1_b': (0.0, 0.8),
     'L0_conv_qkv_b': (0.0, 0.752),
     'L0_conv_proj_b': (0.0, 0.1),
     'L0_conv_ln2_g': (1.0, 0.6),
     'L0_conv_ln2_b': (0.0, 0.8),
     'L0_conv_fc1_b': (0.0, 0.672),
     'L0_conv_fc2_b': (0.0, 0.1)}
    factors = {'L0_conv_qkv_w': 8.0,
     'L0_conv_rpb': 24.907,
     'L0_conv_proj_w': 5.39,
     'L0_conv_fc1_w': 4.338,
     'L0_conv_fc2_w': 3.143}
    for name, (base, spread) in spreads.items():
        noise = np.random.default_rng([zlib.crc32(name.encode()), seed]).standard_normal(out[name].shape)
        drawn = base * np.exp(spread * noise) if base else spread * noise
        out[name] = jnp.asarray(drawn.astype(out[name].dtype))
    for name, factor in factors.items():
        out[name] = (out[name] * factor).astype(out[name].dtype)
    return out
```

```python
from contextlib import ExitStack

import concourse.bass as bass
from concourse import mybir


def swin_block_kernel(nc, x, ln1_g, ln1_b, qkv_w, qkv_b, rpb, proj_w, proj_b,
                      ln2_g, ln2_b, fc1_w, fc1_b, fc2_w, fc2_b, out):
    fp32, bf16 = mybir.dt.float32, mybir.dt.bfloat16
    ALU, ACT, AX = mybir.AluOpType, mybir.ActivationFunctionType, mybir.AxisListType

    B, C, H, W = x.shape
    WS = 8
    NT = WS * WS
    NH = rpb.shape[1]
    HD = C // NH
    G = 128 // C
    NW = W // WS
    TC = WS * W
    HC = C // 2
    NCH = B * H * W // (G * TC)
    NR = NCH // 2
    HID = fc1_w.shape[0]
    SIDE = 2 * WS - 1
    TERMS = [(0, 0), (0, 1), (1, 0), (1, 1), (0, 2), (2, 0)]
    KR = len(TERMS) * HC
    GP = 2 * G
    XP = 4
    READS = 2 * len(TERMS)

    x_v = x.rearrange("(a y) c (r v i) w -> y r a v c (i w)", y=2, v=2, i=WS)
    out_v = out.rearrange("(a y) c (r v i) w -> y r a v c (i w)", y=2, v=2, i=WS)

    ctx = ExitStack()
    with ctx:
        def sb(name, shape, dt=fp32):
            return ctx.enter_context(nc.sbuf_tensor(name, shape, dt))

        def sem(name):
            return ctx.enter_context(nc.semaphore(name))

        parts_dram = [nc.dram_tensor(f"parts{i}", [128, 6 * TC], bf16).ap() for i in range(2)]

        x_sb = sb("x_sb", [128, NCH // 2, 2, TC])
        x1_sb = sb("x1_sb", [128, NCH // 2, 2, TC])
        sq1 = sb("sq1", [128, TC])
        rstd1 = sb("rstd1", [128, TC])
        sq2 = sb("sq2", [128, TC])
        rstd2 = sb("rstd2", [128, TC])
        h1 = sb("h1", [128, 2, NW, NT])
        rest = sb("rest", [128, 2, TC])
        parts = sb("parts", [128, 2, 6, TC], bf16)
        q_in = sb("q_in", [KR, 2, GP, TC], bf16)
        q_st = sb("q_st", [KR, GP, NW, 2, NT], bf16)
        k_st = sb("k_st", [KR, 2, GP, TC], bf16)
        prob = sb("prob", [128, 2, XP, NW, 2, NT])
        prob_t = sb("prob_t", [128, 2, XP, 4, 128])
        v_blk = sb("v_blk", [128, 2, NW, XP, 2 * HC])
        den = sb("den", [128, 4, 2, NT])
        att = sb("att", [128, 2, TC])

        ident = sb("ident", [128, 128])
        mean_m = sb("mean_m", [128, 128])
        cent_m = sb("cent_m", [128, 128])
        ones_v = sb("ones_v", [128, 2 * HC])
        eps = sb("eps", [128, 1])
        head_m = sb("head_m", [KR, 2])
        mx = sb("mx", [128, 2, NW])
        raw_b = sb("raw_b", [NT, WS, WS * NH])
        bias_t = sb("bias_t", [128, 2, WS, WS])
        vec_r = sb("vec_r", [9, G, C])
        vec = sb("vec", [128, 9])
        fc1_bc = sb("fc1_bc", [HID, 1])
        w_nat = sb("w_nat", [3 * C, C])
        p_nat = sb("p_nat", [128, C])
        f1_nat = sb("f1_nat", [HID, C])
        f2_nat = sb("f2_nat", [C, HID])
        w_rep = sb("w_rep", [3 * C, G, C])
        f1_rep = sb("f1_rep", [HID, G, C])
        nat = sb("nat", [128, 3, 128])
        raw_t = sb("raw_t", [128, 4, 128])
        wqk = sb("wqk", [128, 2, 128])
        wv = sb("wv", [128, 2, 2, C])
        wp = sb("wp", [128, 2, 128])
        f1_t = sb("f1_t", [128, HID])
        f1_st = sb("f1_st", [128, G, HID])
        f2_st = sb("f2_st", [HID, C])
        bq = sb("bq", [128, 4])
        fb1 = sb("fb1", [HID, 1])
        hid = prob[:, :, 0:2, :, :, :].rearrange("p u q w v m -> p u (q w v m)").rearrange("p u (g n) -> p u g n", g=G)
        y_sb = sb("y_sb", [128, 2, TC])

        ps = ctx.enter_context(nc.psum_tensor("ps", [128, 8, TC], fp32))
        S_PS = [ps[:, 0, :], ps[:, 1, :]]
        T_PS = [ps[:, 2, :], ps[:, 3, :]]
        FA, FB = ps[:, 4, :], ps[:, 5, :]
        O_PS, D_PS = ps[:, 6, :], ps[:, 7, :]

        x_in = [sem(f"x_in{i}") for i in range(4)]
        w_in = sem("w_in")
        vec_in = sem("vec_in")
        bias_in = sem("bias_in")
        masked = sem("masked")
        ident_ready = sem("ident_ready")
        const_ready = sem("const_ready")
        nat_ready = sem("nat_ready")
        setup_t = sem("setup_t")
        setup_v = sem("setup_v")
        setup_b = sem("setup_b")
        ready = sem("ready")
        centered1, var1_ready = sem("centered1"), sem("var1_ready")
        q_ready, k_ready, v_ready = sem("q_ready"), sem("k_ready"), sem("v_ready")
        scores_ready, transposed = sem("scores_ready"), sem("transposed")
        attended, summed = sem("attended"), sem("summed")
        projected, centered2, var2_ready = sem("projected"), sem("centered2"), sem("var2_ready")
        squared1, log1, rstd1_ready = sem("squared1"), sem("log1"), sem("rstd1_ready")
        squared2, log2, rstd2_ready = sem("squared2"), sem("log2"), sem("rstd2_ready")
        h1_ready = sem("h1_ready")
        part0, resid, part1, part2 = sem("part0"), sem("resid"), sem("part1"), sem("part2")
        v_low, v_high = sem("v_low"), sem("v_high")
        biased, maxed, shifted, expd = sem("biased"), sem("maxed"), sem("shifted"), sem("expd")
        prob_copied, divided = sem("prob_copied"), sem("divided")
        den_log, den_ready = sem("den_log"), sem("den_ready")
        x1_ready, h2_ready = sem("x1_ready"), sem("h2_ready")
        parts_out = [sem(f"parts_out{i}") for i in range(2)]
        stacks_in = [sem(f"stacks_in{i}") for i in range(2)]
        hidden_ready, gelu_ready, down_ready, y_ready = sem("hidden_ready"), sem("gelu_ready"), sem("down_ready"), sem("y_ready")
        stored = [sem("stored0"), sem("stored1")]

        block = ctx.enter_context(nc.Block())

        S_LAG, T_LAG, P_LAG = 1, 2, 3

        def chunk(jt, ut, lag):
            return jt + (ut - lag) // 2, (ut - lag) % 2

        def live(t, lag):
            return 0 <= t - lag < NCH

        def steps(eng, step):
            full0 = P_LAG + P_LAG % 2
            for t in range(full0):
                step(t // 2, t % 2, [live(t, lag) for lag in range(4)])
            with eng.Fori(full0 // 2, NCH // 2) as jt:
                for u in range(2):
                    step(jt, u, [True] * 4)
            for t in range(NCH, NCH + P_LAG):
                step(t // 2, t % 2, [live(t, lag) for lag in range(4)])

        def done(c, per, k):
            j, u = c
            return j * (2 * per) + (u * per + k)

        def first(c, n):
            j, u = c
            return isinstance(j, int) and 2 * j + u < n

        def last(c):
            j, u = c
            return isinstance(j, int) and 2 * j + u == NCH - 1

        def cols(buf, c):
            j, u = c
            if isinstance(j, int):
                return buf[:, j, u, :]
            return buf[:, bass.ds(j, 1), u, :].rearrange("p o n -> p (o n)")

        @block.sync
        def _(sp):
            def load_x(c):
                for a in range(2):
                    for v in range(2):
                        g = 2 * a + v
                        sp.dma_start(x_sb[C * g:C * (g + 1), c // 2, c % 2, :],
                                     x_v[c // NR, c % NR, a, v, :, :]).then_inc(x_in[min(c, 3)], 16)

            load_x(0)
            sp.dma_start(w_nat[:, :], qkv_w).then_inc(w_in, 16)
            for g in range(G):
                sp.dma_start(p_nat[C * g:C * (g + 1), :], proj_w).then_inc(w_in, 16)
            load_x(1)
            sp.dma_start(f1_nat[:, :], fc1_w).then_inc(w_in, 16)
            sp.dma_start(f2_nat[:, :], fc2_w).then_inc(w_in, 16)
            for c in range(2, NCH):
                load_x(c)

            def restack(jt, u, on):
                if not on[0]:
                    return
                c = (jt, u)
                dram = parts_dram[u].rearrange("(g c) (s n) -> s c g n", c=HC, s=6)
                sp.wait_ge(part0, done(c, 2, 2))
                sp.wait_ge(part1, done(c, 2, 2))
                sp.wait_ge(part2, done(c, 2, 2))
                sp.dma_start(parts_dram[u], parts[:, u, :, :].rearrange("p s n -> p (s n)")).then_inc(parts_out[u], 16)
                sp.wait_ge(parts_out[u], jt * 16 + 16)
                for t, (qi, ki) in enumerate(TERMS):
                    sp.dma_start(q_in[HC * t:HC * (t + 1), u, :, :], dram[qi]).then_inc(stacks_in[u], 16)
                    sp.dma_start(k_st[HC * t:HC * (t + 1), u, :, :], dram[3 + ki]).then_inc(stacks_in[u], 16)

            steps(sp, restack)

            for c in range(NCH):
                sp.wait_ge(y_ready, c + 1)
                for a in range(2):
                    for v in range(2):
                        g = 2 * a + v
                        sp.dma_start(out_v[c // NR, c % NR, a, v, :, :], y_sb[C * g:C * (g + 1), c % 2, :])\
                          .then_inc(stored[c % 2], 16)
            for u in range(2):
                sp.wait_ge(stored[u], 16 * G * NCH // 2)

        @block.gpsimd
        def _(pool):
            pool.memset(ident[:, :], 0.0).then_inc(ident_ready, 1)
            pool.wait_ge(ident_ready, 1)
            pool.affine_select(out=ident[:, :], in_=ident[:, :], compare_op=ALU.not_equal, fill=1.0,
                               base=0, pattern=[[-1, 128]], channel_multiplier=1).then_inc(ident_ready, 1)
            rows = [ln1_g, ln1_b, qkv_b[0:C], qkv_b[C:2 * C], qkv_b[2 * C:3 * C], proj_b, ln2_g, ln2_b, fc2_b]
            for i, vector in enumerate(rows):
                pool.dma_start(vec_r[i:i + 1, :, :], bass.AP(vector.tensor, vector.offset, [[C, 1], [0, G], [1, C]]))\
                    .then_inc(vec_in, 16)
            pool.dma_start(fc1_bc[:, :], fc1_b.rearrange("(p o) -> p o", o=1)).then_inc(vec_in, 16)
            for ny in range(WS):
                pool.dma_start(raw_b[WS * ny:WS * (ny + 1), :, :],
                               bass.AP(rpb.tensor, rpb.offset + ny * SIDE * NH,
                                       [[NH, WS], [SIDE * NH, WS], [1, WS * NH]])).then_inc(bias_in, 16)

            def step(jt, u, on):
                if on[0]:
                    c = (jt, u)
                    for i in range(2):
                        pool.wait_ge(part1, done(c, 2, i + 1))
                        pool.tensor_tensor(parts[:, u, 3 * i + 2, :], rest[:, i, :], parts[:, u, 3 * i + 1, :],
                                           ALU.subtract).then_inc(part2, 1)
                return

            def step_s(jt, u, on):
                if on[S_LAG]:
                    c = chunk(jt, u, S_LAG)
                    for s in range(GP):
                        pool.wait_ge(maxed, done(c, GP, s + 1))
                        tile = prob[:, c[1], s // 2, :, s % 2, :]
                        pool.tensor_tensor(tile, tile, mx[:, s % 2, :].unsqueeze(2).to_broadcast([128, NW, NT]),
                                           ALU.subtract).then_inc(shifted, 1)
                        if s == 5:
                            step(jt, u, on)
                else:
                    step(jt, u, on)

            steps(pool, step_s)

        @block.scalar
        def _(act):
            act.preload_act_table_set("natural_log_exp_and_others")

            def exp_tile(c, s):
                act.wait_ge(shifted, done(c, GP, s + 1))
                tile = prob[:, c[1], s // 2, :, s % 2, :]
                act.activation(tile, tile, ACT.Exp).then_inc(expd, 1)

            def copy_bank(c, k):
                act.wait_ge(transposed, done(c, 8, k + 1))
                if k % 4 == 0 and not first(c, 1):
                    act.wait_ge(summed, done(c, 2, k // 4 + 1) - 2)
                act.activation(prob_t[:, k // 4, k % 4, :, :], T_PS[k % 2].rearrange("p (w n) -> p w n", n=128),
                               ACT.Copy).then_inc(prob_copied, 1)

            def invert_den(c, half):
                act.wait_ge(summed, done(c, 2, half + 1))
                if not (first(c, 1) and half == 0):
                    act.wait_ge(divided, done(c, 2, half))
                act.activation(den[:, :, :, :], D_PS.rearrange("p (w h n) -> p w h n", h=2, n=NT), ACT.Ln)\
                   .then_inc(den_log, 1)
                act.wait_ge(den_log, done(c, 2, half + 1))
                act.activation(den[:, :, :, :], den[:, :, :, :], ACT.Exp, scale=-1.0).then_inc(den_ready, 1)

            def step(jt, u, on):
                f, s, b, p = (chunk(jt, u, lag) for lag in range(4))
                for k in range(8):
                    if k < 2 and on[T_LAG]:
                        exp_tile(b, 6 + k)
                    if k >= 2 and on[S_LAG]:
                        exp_tile(s, k - 2)
                    if on[T_LAG]:
                        copy_bank(b, k)
                    if k == 0 and on[0]:
                        act.wait_ge(centered1, done(f, 1, 1))
                        if not first(f, 1):
                            act.wait_ge(var1_ready, done(f, 1, 0))
                        act.activation(sq1[:, :], FA, ACT.Square).then_inc(squared1, 1)
                    if k == 0 and on[P_LAG]:
                        invert_den(p, 1)
                    if k == 1 and on[0]:
                        act.wait_ge(var1_ready, done(f, 1, 1))
                        if not first(f, 1):
                            act.wait_ge(h1_ready, done(f, 1, 0))
                        act.activation(rstd1[:, :], FB, ACT.Ln, bias=eps[:, :]).then_inc(log1, 1)
                        act.wait_ge(log1, done(f, 1, 1))
                        act.activation(rstd1[:, :], rstd1[:, :], ACT.Exp, scale=-0.5).then_inc(rstd1_ready, 1)
                    if k == 4 and on[0]:
                        for i, (bank, made) in enumerate(((FA, q_ready), (FB, k_ready))):
                            act.wait_ge(made, done(f, 1, 1))
                            if not first(f, 2):
                                act.wait_ge(parts_out[f[1]], f[0] * 16)
                            act.activation(parts[:, f[1], 3 * i, :], bank, ACT.Identity, bias=bq[:, i:i + 1])\
                               .then_inc(part0, 1)
                    if k == 5 and on[P_LAG]:
                        act.wait_ge(centered2, done(p, 1, 1))
                        if not first(p, 1):
                            act.wait_ge(var2_ready, done(p, 1, 0))
                        act.activation(sq2[:, :], D_PS, ACT.Square).then_inc(squared2, 1)
                    if k == 6 and on[P_LAG]:
                        act.wait_ge(var2_ready, done(p, 1, 1))
                        if not first(p, 1):
                            act.wait_ge(h2_ready, done(p, 1, 0))
                        act.activation(rstd2[:, :], O_PS, ACT.Ln, bias=eps[:, :]).then_inc(log2, 1)
                        act.wait_ge(log2, done(p, 1, 1))
                        act.activation(rstd2[:, :], rstd2[:, :], ACT.Exp, scale=-0.5).then_inc(rstd2_ready, 1)
                    if k == 7 and on[S_LAG]:
                        act.wait_ge(v_ready, done(s, 1, 1))
                        if not first(s, 2):
                            act.wait_ge(attended, done(s, 2, 0) - 2)
                        act.activation(v_blk[0:64, s[1], :, :, 0:HC],
                                       FA[0:64].rearrange("p (w q e) -> p w q e", w=NW, q=XP), ACT.Copy)\
                           .then_inc(v_low, 1)
                    if k == 7 and on[T_LAG]:
                        invert_den(b, 0)

            act.wait_ge(ready, 1)
            steps(act, step)

            def gelu(i2, u):
                for g in range(G):
                    act.wait_ge(hidden_ready, (i2 * 2 + u) * G + g + 1)
                    if not (isinstance(i2, int) and i2 == 0):
                        act.wait_ge(down_ready, (i2 * 2 + (u - 1)) * G + (g + 1 - G))
                    act.activation(hid[:, u, g, :], ps[:, g, :], ACT.Gelu, bias=fb1[:, :]).then_inc(gelu_ready, 1)

            gelu(0, 0)
            gelu(0, 1)
            with act.Fori(1, NCH // 2) as i2:
                gelu(i2, 0)
                gelu(i2, 1)

        @block.vector
        def _(dve):
            n_setup = [0]

            def link(ins):
                n_setup[0] += 1
                ins.then_inc(setup_v, 1)
                dve.wait_ge(setup_v, n_setup[0])

            dve.memset(mean_m[:, :], 0.0)
            dve.memset(ones_v[:, :], 0.0)
            dve.memset(eps[:, :], 1e-5)
            dve.memset(raw_t[:, :, :], 0.0)
            dve.memset(nat[:, :, :], 0.0)
            dve.memset(f1_st[:, :, :], 0.0)
            link(dve.memset(v_blk[:, :, :, :, :], 0.0))
            for g in range(G):
                dve.memset(mean_m[C * g:C * (g + 1), C * g:C * (g + 1)], 1.0 / C)
            for v in range(2):
                link(dve.memset(ones_v[64 * v:64 * (v + 1), HC * v:HC * (v + 1)], 1.0))
            dve.wait_ge(ident_ready, 2)
            dve.tensor_tensor(cent_m[:, :], ident[:, :], mean_m[:, :], ALU.subtract).then_inc(const_ready, 1)
            dve.reduce_sum(head_m[:, :], ident[0:KR, 0:KR].rearrange("p (t h d) -> p h t d", h=2, d=HD), AX.XY)
            dve.wait_ge(w_in, 16 * 7)
            dve.tensor_copy(w_rep[:, :, :], w_nat[:, :].unsqueeze(1).to_broadcast([3 * C, G, C]))
            for a in range(2):
                for v in range(2):
                    r = slice(C * (2 * a + v), C * (2 * a + v + 1))
                    dve.tensor_copy(nat[r, 0, r], p_nat[r, :])
                    for hh in range(2):
                        dst = nat[r, 1 + hh, :].rearrange("p (x q v e) -> p x q v e", x=2, q=2, v=2)
                        src = p_nat[r, :].rearrange("p (q e) -> p q e", q=2)
                        link(dve.tensor_copy(dst[:, a, :, v, HD * hh:HD * (hh + 1)],
                                             src[:, :, HD * hh:HD * (hh + 1)]))
            dve.tensor_copy(f1_rep[:, :, :], f1_nat[:, :].unsqueeze(1).to_broadcast([HID, G, C])).then_inc(nat_ready, 1)
            dve.wait_ge(setup_t, 1)
            dve.tensor_copy(vec[:, :], ps[:, 0, 0:9])
            for g in range(G):
                r = slice(C * g, C * (g + 1))
                dve.tensor_copy(raw_t[r, 0:3, r], ps[r, 1, 0:3 * C].rearrange("p (s o) -> p s o", s=3))
            dve.tensor_copy(raw_t[:, 3, :], ps[:, 2, 0:128])
            dve.tensor_copy(wp[:, :, :], ps[:, 2, 128:384].rearrange("p (h o) -> p h o", h=2))
            dve.tensor_copy(f1_t[:, :], ps[:, 3, 0:HID])
            link(dve.tensor_copy(f2_st[:, :], ps[:, 4, 0:C]))
            dve.tensor_scalar(wqk[:, 0, :], raw_t[:, 0, :], vec[:, 0:1], HD ** -0.5, ALU.mult, ALU.mult)
            dve.tensor_scalar(wqk[:, 1, :], raw_t[:, 1, :], vec[:, 0:1], None, ALU.mult)
            dve.tensor_scalar(wv[:, :, :, :].rearrange("p v x e -> p x v e"),
                              raw_t[:, 2, :].rearrange("p (x v e) -> p x v e", x=2, v=2), vec[:, 0:1], None, ALU.mult)
            for g in range(G):
                r = slice(C * g, C * (g + 1))
                ins = dve.tensor_scalar(f1_st[r, g, :], f1_t[r, :], vec[r, 6:7], None, ALU.mult)
            ins.then_inc(setup_b, 1)
            dve.wait_ge(setup_t, 2)
            dve.tensor_scalar(bq[:, 0:1], ps[:, 5, 0:1], vec[:, 2:3], HD ** -0.5, ALU.add, ALU.mult)
            dve.tensor_scalar(bq[:, 1:2], ps[:, 5, 1:2], vec[:, 3:4], None, ALU.add)
            dve.tensor_scalar(bq[:, 2:3], ps[:, 5, 2:3], vec[:, 4:5], None, ALU.add).then_inc(setup_b, 1)
            dve.tensor_scalar(fb1[:, :], ps[:, 5, 3:4], fc1_bc[:, :], None, ALU.add)
            dve.wait_ge(setup_t, 3)
            link(dve.tensor_scalar(bq[:, 3:4], ps[:, 6, 0:1], vec[:, 5:6], None, ALU.add))
            dve.wait_ge(bias_in, 16 * WS)
            table = raw_b[:, :, :].rearrange("p y (x h) -> p y x h", h=NH)
            for hh in range(2):
                for pr in range(2):
                    ins = dve.tensor_copy(bias_t[NT * hh:NT * (hh + 1), pr, :, :], table[:, ::-1, ::-1, 2 * pr + hh])
            ins.then_inc(ready, 1)
            dve.wait_ge(ready, 1)

            bias_pair = bias_t[:, :, :, :].rearrange("p q y x -> p q (y x)")

            def divide(c, half):
                dve.wait_ge(attended, done(c, 2, half + 1))
                dve.wait_ge(den_ready, done(c, 2, half + 1))
                if half == 0 and not first(c, 1):
                    dve.wait_ge(projected, done(c, 1, 0))
                for hh in range(2):
                    dst = att[:, hh, :].rearrange("p (i w j) -> p w i j", i=WS, j=WS)[:, 4 * half:4 * half + 4]
                    src = O_PS.rearrange("p (w h i j) -> p h w i j", w=4, h=2, i=WS)[:, hh]
                    ins = dve.tensor_tensor(dst, src, den[:, :, hh, :].rearrange("p w (i j) -> p w i j", i=WS),
                                            ALU.mult)
                ins.then_inc(divided, 1)

            def split(f, i, bank, made):
                dve.wait_ge(made, done(f, 1, 1))
                dve.wait_ge(part0, done(f, 2, i + 1))
                if not first(f, 1):
                    dve.wait_ge(part2, done(f, 2, i + 1) - 2)
                dve.scalar_tensor_tensor(out=rest[:, i, :], in0=bank, scalar=bq[:, i:i + 1],
                                         in1=parts[:, f[1], 3 * i, :], op0=ALU.add, op1=ALU.subtract)\
                   .then_inc(resid, 1)
                dve.wait_ge(resid, done(f, 2, i + 1))
                if not first(f, 2):
                    dve.wait_ge(parts_out[f[1]], f[0] * 16)
                dve.tensor_copy(parts[:, f[1], 3 * i + 1, :], rest[:, i, :]).then_inc(part1, 1)

            def step(jt, u, on):
                f, s, b, p = (chunk(jt, u, lag) for lag in range(4))
                for k in range(8):
                    if on[S_LAG]:
                        if k == 0:
                            dve.wait_ge(stacks_in[s[1]], s[0] * (16 * READS) + 16 * READS)
                        for n in ([0, 1] if k == 0 else [k + 1] if k < 7 else []):
                            gp = (2 * (n // 4) + n % 2) * 2 + (n // 2) % 2
                            if not first(s, 1):
                                dve.wait_ge(scores_ready, done(s, GP, n + 1) - GP)
                            for hh in range(2):
                                ins = dve.tensor_scalar(q_st[:, gp, :, hh, :],
                                                        q_in[:, s[1], gp, :].rearrange("p (w n) -> p w n", n=NT),
                                                        head_m[:, hh:hh + 1], None, ALU.mult)
                            ins.then_inc(masked, 1)
                        tile = prob[:, s[1], k // 2, :, k % 2, :]
                        pair = (k // 2) % 2
                        dve.wait_ge(scores_ready, done(s, GP, k + 1))
                        if k == 0 and not first(s, 2):
                            dve.wait_ge(transposed, done(s, 8, 0) - 8)
                        dve.tensor_tensor(tile, S_PS[k % 2].rearrange("p (w m) -> p w m", m=NT),
                                          bias_pair[:, pair, :].unsqueeze(1).to_broadcast([128, NW, NT]),
                                          ALU.add).then_inc(biased, 1)
                        dve.wait_ge(biased, done(s, GP, k + 1))
                        if not (first(s, 1) and k < 2):
                            dve.wait_ge(shifted, done(s, GP, k + 1) - 2)
                        dve.reduce_max(mx[:, k % 2, :], tile, AX.X).then_inc(maxed, 1)
                    if k == 1 and on[P_LAG]:
                        divide(p, 1)
                    if k == 2 and on[0]:
                        dve.wait_ge(rstd1_ready, done(f, 1, 1))
                        if not first(f, 2):
                            dve.wait_ge(v_ready, done(f, 1, 0) - 1)
                        dve.tensor_tensor(h1[:, f[1], :, :].rearrange("p w (i j) -> p w i j", i=WS),
                                          FA.rearrange("p (i w j) -> p w i j", i=WS, j=WS),
                                          rstd1[:, :].rearrange("p (i w j) -> p w i j", i=WS, j=WS),
                                          ALU.mult).then_inc(h1_ready, 1)
                    if k == 3 and on[P_LAG]:
                        dve.wait_ge(projected, done(p, 1, 1))
                        dve.scalar_tensor_tensor(out=cols(x1_sb, p), in0=O_PS, scalar=bq[:, 3:4],
                                                 in1=cols(x_sb, p), op0=ALU.add, op1=ALU.add).then_inc(x1_ready, 1)
                    if k == 4 and on[0]:
                        split(f, 0, FA, q_ready)
                    if k == 5 and on[0]:
                        split(f, 1, FB, k_ready)
                    if k == 7 and on[P_LAG]:
                        dve.wait_ge(rstd2_ready, done(p, 1, 1))
                        dve.tensor_tensor(cols(x_sb, p), D_PS, rstd2[:, :], ALU.mult).then_inc(h2_ready, 1)
                    if k == 7 and on[S_LAG]:
                        dve.wait_ge(v_ready, done(s, 1, 1))
                        if not first(s, 2):
                            dve.wait_ge(attended, done(s, 2, 0) - 2)
                        dve.tensor_copy(v_blk[64:128, s[1], :, :, HC:2 * HC],
                                        FA[64:128].rearrange("p (w q e) -> p w q e", w=NW, q=XP)).then_inc(v_high, 1)
                    if k == 7 and on[T_LAG]:
                        divide(b, 0)

            steps(dve, step)

            def finish(i2, u):
                n = i2 * 2 + u
                dve.wait_ge(down_ready, (i2 * 2 + u) * G + G)
                if not (isinstance(i2, int) and i2 == 0):
                    dve.wait_ge(stored[u], i2 * (16 * G))
                dve.scalar_tensor_tensor(out=y_sb[:, u, :], in0=ps[:, 4 + u, :], scalar=vec[:, 8:9],
                                         in1=cols(x1_sb, (i2, u)), op0=ALU.add, op1=ALU.add).then_inc(y_ready, 1)

            finish(0, 0)
            finish(0, 1)
            with dve.Fori(1, NCH // 2) as i2:
                finish(i2, 0)
                finish(i2, 1)

        @block.tensor
        def _(pe):
            pe.wait_ge(const_ready, 1)
            pe.wait_ge(w_in, 16 * 7)
            pe.wait_ge(vec_in, 16 * 10)
            pe.wait_ge(nat_ready, 1)
            pe.transpose(ps[:, 0, 0:9], vec_r[:, :, :].rearrange("p g c -> p (g c)"), ident[0:9, 0:9])
            pe.transpose(ps[:, 1, 0:3 * C], w_rep[:, :, :].rearrange("p g c -> p (g c)"), ident[0:3 * C, 0:3 * C])
            for i in range(3):
                pe.transpose(ps[:, 2, 128 * i:128 * (i + 1)], nat[:, i, :], ident[:, :])
            pe.transpose(ps[:, 3, 0:HID], f1_rep[:, :, :].rearrange("p g c -> p (g c)"), ident[:, :])
            pe.transpose(ps[:, 4, 0:C], f2_nat[:, :], ident[0:C, 0:C]).then_inc(setup_t, 1)
            pe.wait_ge(setup_b, 1)
            for i in range(3):
                pe.matmul(ps[:, 5, i:i + 1], raw_t[:, i, :], vec[:, 1:2], start=True, stop=True)
            pe.matmul(ps[:, 5, 3:4], f1_t[0:C, :], vec[0:C, 7:8], start=True, stop=True).then_inc(setup_t, 1)
            pe.wait_ge(setup_b, 2)
            pe.matmul(ps[:, 6, 0:1], raw_t[:, 3, :], bq[:, 2:3], start=True, stop=True).then_inc(setup_t, 1)
            pe.wait_ge(ready, 1)

            def attend(c, half):
                pe.wait_ge(prob_copied, done(c, 8, 4 * half + 4))
                pe.wait_ge(v_low, done(c, 1, 1))
                pe.wait_ge(v_high, done(c, 1, 1))
                if half == 1:
                    pe.wait_ge(divided, done(c, 2, 1))
                elif not first(c, 1):
                    pe.wait_ge(log2, done(c, 1, 0))
                for w in range(4):
                    for q in range(XP):
                        ins = pe.matmul(O_PS[32 * q:32 * (q + 1), 128 * w:128 * (w + 1)],
                                        v_blk[:, c[1], 4 * half + w, q, :], prob_t[:, half, q, w, :],
                                        start=True, stop=True, tile_position=(0, 32 * q))
                ins.then_inc(attended, 1)
                if half == 0 and not first(c, 1):
                    pe.wait_ge(h2_ready, done(c, 1, 0))
                for q in range(XP):
                    ins = pe.matmul(D_PS[32 * q:32 * (q + 1), :], ones_v[:, :],
                                    prob_t[:, half, q, :, :].rearrange("p w n -> p (w n)"),
                                    start=True, stop=True, tile_position=(0, 32 * q))
                ins.then_inc(summed, 1)

            def step(jt, u, on):
                f, s, b, p = (chunk(jt, u, lag) for lag in range(4))
                for k in range(8):
                    if k == 0 and on[0]:
                        if isinstance(jt, int) and 2 * jt + u < 3:
                            pe.wait_ge(x_in[2 * jt + u], 16 * G)
                        elif isinstance(jt, int) and 2 * jt + u == 3:
                            pe.wait_ge(x_in[3], 16 * G * (NCH - 3))
                        if first(f, 2) and not first(f, 1):
                            pe.wait_ge(resid, 1)
                        if not first(f, 2):
                            pe.wait_ge(v_low, done(f, 1, 0) - 1)
                            pe.wait_ge(v_high, done(f, 1, 0) - 1)
                        pe.matmul(FA, cent_m[:, :], cols(x_sb, f), start=True, stop=True).then_inc(centered1, 1)
                    if k == 0 and on[P_LAG]:
                        attend(p, 1)
                    if on[S_LAG]:
                        gp = (2 * (k // 4) + k % 2) * 2 + (k // 2) % 2
                        if k == 0:
                            pe.wait_ge(stacks_in[s[1]], s[0] * (16 * READS) + 16 * READS)
                        if not (first(s, 1) and k < 2):
                            pe.wait_ge(biased, done(s, GP, k + 1) - 2)
                        pe.wait_ge(masked, done(s, GP, k + 1))
                        for w in range(NW):
                            ins = pe.matmul(S_PS[k % 2][:, NT * w:NT * (w + 1)],
                                            q_st[:, gp, w, :, :].rearrange("p h n -> p (h n)"),
                                            k_st[:, s[1], gp, NT * w:NT * (w + 1)], start=True, stop=True)
                        ins.then_inc(scores_ready, 1)
                    if on[T_LAG]:
                        half, q = k // 4, k % 4
                        if half == 0:
                            pe.wait_ge(expd, done(b, GP, 2 * q + 2))
                        if not (first(b, 1) and k < 2):
                            pe.wait_ge(prob_copied, done(b, 8, k + 1) - 2)
                        for w in range(4):
                            ins = pe.transpose(T_PS[k % 2][:, 128 * w:128 * (w + 1)],
                                               prob[:, b[1], q, 4 * half + w, :, :].rearrange("p v m -> p (v m)"),
                                               ident[:, :])
                        ins.then_inc(transposed, 1)
                    if k == 1 and on[0]:
                        pe.wait_ge(squared1, done(f, 1, 1))
                        if not first(f, 1):
                            pe.wait_ge(resid, done(f, 2, 0))
                        pe.matmul(FB, mean_m[:, :], sq1[:, :], start=True, stop=True).then_inc(var1_ready, 1)
                    if k == 2 and on[P_LAG]:
                        pe.wait_ge(divided, done(p, 2, 2))
                        for hh in range(2):
                            ins = pe.matmul(O_PS, wp[:, hh, :], att[:, hh, :], start=(hh == 0), stop=(hh == 1))
                        ins.then_inc(projected, 1)
                    if k == 3 and on[0]:
                        pe.wait_ge(h1_ready, done(f, 1, 1))
                        hv = h1[:, f[1], :, :].rearrange("p w n -> p (w n)")
                        pe.matmul(FA, wqk[:, 0, :], hv, start=True, stop=True).then_inc(q_ready, 1)
                        pe.matmul(FB, wqk[:, 1, :], hv, start=True, stop=True).then_inc(k_ready, 1)
                    if k == 4 and on[P_LAG]:
                        pe.wait_ge(x1_ready, done(p, 1, 1))
                        pe.matmul(D_PS, cent_m[:, :], cols(x1_sb, p), start=True, stop=True).then_inc(centered2, 1)
                    if k == 5 and on[P_LAG]:
                        pe.wait_ge(squared2, done(p, 1, 1))
                        pe.matmul(O_PS, mean_m[:, :], sq2[:, :], start=True, stop=True).then_inc(var2_ready, 1)
                    if k == 6 and on[S_LAG]:
                        if on[0]:
                            pe.wait_ge(resid, done(f, 2, 1))
                        else:
                            pe.wait_ge(v_low, done(s, 1, 0))
                            pe.wait_ge(v_high, done(s, 1, 0))
                        for w in range(NW):
                            for v in range(2):
                                ins = pe.matmul(FA[64 * v:64 * (v + 1), 64 * w:64 * (w + 1)], h1[:, s[1], w, :],
                                                wv[:, v, :, :].rearrange("p x e -> p (x e)"), start=True, stop=True,
                                                tile_position=(0, 64 * v))
                        ins.then_inc(v_ready, 1)
                    if k == 7 and on[T_LAG]:
                        attend(b, 0)

            steps(pe, step)

            pe.wait_ge(h2_ready, NCH)
            pe.wait_ge(log2, NCH)
            pe.wait_ge(prob_copied, 8 * NCH)

            def up(i2, u, g):
                if not (isinstance(i2, int) and 2 * i2 + u == 0):
                    pe.wait_ge(gelu_ready, (i2 * 2 + u) * G + (g + 1 - G))
                pe.matmul(ps[:, g, :], f1_st[:, g, :], cols(x_sb, (i2, u)), start=True, stop=True)\
                  .then_inc(hidden_ready, 1)

            def down(i2, u, g):
                if g == 0 and not (isinstance(i2, int) and i2 == 0):
                    pe.wait_ge(y_ready, i2 * 2 + (u - 1))
                pe.wait_ge(gelu_ready, (i2 * 2 + u) * G + g + 1)
                pe.matmul(ps[C * g:C * (g + 1), 4 + u, :], f2_st[:, :], hid[:, u, g, :], start=True, stop=True,
                          tile_position=(0, C * g)).then_inc(down_ready, 1)

            for g in range(G):
                up(0, 0, g)
            for g in range(G):
                up(0, 1, g)
                down(0, 0, g)
            with pe.Fori(1, NCH // 2) as i2:
                for g in range(G):
                    up(i2, 0, g)
                    down(i2 - 1, 1, g)
                for g in range(G):
                    up(i2, 1, g)
                    down(i2, 0, g)
            for g in range(G):
                down(NCH // 2 - 1, 1, g)


_INS = ['x', 'L0_conv_ln1_g', 'L0_conv_ln1_b', 'L0_conv_qkv_w', 'L0_conv_qkv_b', 'L0_conv_rpb', 'L0_conv_proj_w',
        'L0_conv_proj_b', 'L0_conv_ln2_g', 'L0_conv_ln2_b', 'L0_conv_fc1_w', 'L0_conv_fc1_b', 'L0_conv_fc2_w',
        'L0_conv_fc2_b']


def kernel(**inputs):
    import numpy as _np
    import concourse.bacc as _bacc
    from concourse import mybir as _mybir
    from concourse.bass_utils import run_bass_kernel_spmd as _run

    nc = _bacc.Bacc("TRN2", target_bir_lowering=False, num_devices=1)
    arrays, args = {}, []
    for name in _INS:
        a = _np.ascontiguousarray(inputs[name])
        arrays[f"in_{name}_dram"] = a
        args.append(nc.dram_tensor(f"in_{name}_dram", a.shape, _mybir.dt.from_np(a.dtype), kind="ExternalInput").ap())
    shape = _np.shape(inputs['x'])
    args.append(nc.dram_tensor("out_0_dram", shape, _mybir.dt.float32, kind="ExternalOutput").ap())
    swin_block_kernel(nc, *args)
    r = _run(nc, [arrays], core_ids=[0])
    return r.results[0]["out_0_dram"]
```

```python
from contextlib import ExitStack

import concourse.bass as bass
from concourse import mybir


def swin_block_kernel(nc, x, ln1_g, ln1_b, qkv_w, qkv_b, rpb, proj_w, proj_b,
                      ln2_g, ln2_b, fc1_w, fc1_b, fc2_w, fc2_b, out):
    fp32, bf16 = mybir.dt.float32, mybir.dt.bfloat16
    ALU, ACT, AX = mybir.AluOpType, mybir.ActivationFunctionType, mybir.AxisListType

    B, C, H, W = x.shape
    WS = 8
    NT = WS * WS
    NH = rpb.shape[1]
    HD = C // NH
    G = 128 // C
    NW = W // WS
    TC = WS * W
    HC = C // 2
    NCH = B * H * W // (G * TC)
    NR = NCH // 2
    HID = fc1_w.shape[0]
    SIDE = 2 * WS - 1
    TERMS = [(0, 0), (1, 0), (2, 0), (0, 1), (1, 1), (0, 2)]
    RUNS = [(0, 3, 0, 0), (3, 2, 0, 1), (5, 1, 0, 2)]
    HR = len(TERMS) * HD
    KR = 2 * HR
    GP = 2 * G
    XP = 4
    READS = 2 * 2 * len(RUNS)

    x_v = x.rearrange("(a y) c (r v i) w -> y r a v c (i w)", y=2, v=2, i=WS)
    out_v = out.rearrange("(a y) c (r v i) w -> y r a v c (i w)", y=2, v=2, i=WS)

    ctx = ExitStack()
    with ctx:
        def sb(name, shape, dt=fp32):
            return ctx.enter_context(nc.sbuf_tensor(name, shape, dt))

        def sem(name):
            return ctx.enter_context(nc.semaphore(name))

        parts_dram = [[nc.dram_tensor(f"parts_{n}{i}", [3, HC, GP, TC], bf16).ap() for n in "qk"] for i in range(2)]

        x_sb = sb("x_sb", [128, NCH // 2, 2, TC])
        x1_sb = sb("x1_sb", [128, NCH // 2, 2, TC])
        sq1 = sb("sq1", [128, TC])
        rstd1 = sb("rstd1", [128, TC])
        sq2 = sb("sq2", [128, TC])
        rstd2 = sb("rstd2", [128, TC])
        h1 = sb("h1", [128, 2, NW, NT])
        rest = sb("rest", [128, 2, TC])
        parts = sb("parts", [128, 2, 2, 3, TC], bf16)
        q_st = sb("q_st", [KR, 2, GP, 2, TC], bf16)
        k_st = sb("k_st", [KR, 2, GP, TC], bf16)
        prob = sb("prob", [128, 2, XP, NW, 2, NT])
        prob_t = sb("prob_t", [128, 2, XP, 4, 128])
        v_blk = sb("v_blk", [128, 2, NW, XP, 2 * HC])
        den = sb("den", [128, 4, 2, NT])
        att = sb("att", [128, 2, TC])

        ident = sb("ident", [128, 128])
        mean_m = sb("mean_m", [128, 128])
        cent_m = sb("cent_m", [128, 128])
        ones_v = sb("ones_v", [128, 2 * HC])
        eps = sb("eps", [128, 1])
        mx = sb("mx", [128, 2, NW])
        raw_b = sb("raw_b", [NT, WS, WS * NH])
        bias_t = sb("bias_t", [128, 2, WS, WS])
        vec_r = sb("vec_r", [9, G, C])
        vec = sb("vec", [128, 9])
        fc1_bc = sb("fc1_bc", [HID, 1])
        p_nat = sb("p_nat", [128, C])
        f2_nat = sb("f2_nat", [C, HID])
        w_rep = sb("w_rep", [3 * C, G, C])
        f1_rep = sb("f1_rep", [HID, G, C])
        nat = sb("nat", [128, 3, 128])
        raw_t = sb("raw_t", [128, 4, 128])
        wqk = sb("wqk", [128, 2, 128])
        wv = sb("wv", [128, 2, 2, C])
        wp = sb("wp", [128, 2, 128])
        f1_t = sb("f1_t", [128, HID])
        f1_st = sb("f1_st", [128, G, HID])
        f2_st = sb("f2_st", [HID, C])
        bq = sb("bq", [128, 4])
        fb1 = sb("fb1", [HID, 1])
        hid = prob[:, :, 0:2, :, :, :].rearrange("p u q w v m -> p u (q w v m)").rearrange("p u (g n) -> p u g n", g=G)
        y_sb = sb("y_sb", [128, 2, TC])

        ps = ctx.enter_context(nc.psum_tensor("ps", [128, 8, TC], fp32))
        S_PS = [ps[:, 0, :], ps[:, 1, :]]
        T_PS = [ps[:, 2, :], ps[:, 3, :]]
        FA, FB = ps[:, 4, :], ps[:, 5, :]
        O_PS, D_PS = ps[:, 6, :], ps[:, 7, :]

        x_in = [sem(f"x_in{i}") for i in range(4)]
        w_in = sem("w_in")
        late_in = sem("late_in")
        bias_in = sem("bias_in")
        cleared = sem("cleared")
        ident_ready = sem("ident_ready")
        const_ready = sem("const_ready")
        blank = sem("blank")
        nat_ready = sem("nat_ready")
        setup_t = sem("setup_t")
        setup_v = sem("setup_v")
        setup_b = sem("setup_b")
        weights_ready = sem("weights_ready")
        table_ready = sem("table_ready")
        centered1, var1_ready = sem("centered1"), sem("var1_ready")
        q_ready, k_ready, v_ready = sem("q_ready"), sem("k_ready"), sem("v_ready")
        scores_ready, transposed = sem("scores_ready"), sem("transposed")
        attended, summed = sem("attended"), sem("summed")
        projected, centered2, var2_ready = sem("projected"), sem("centered2"), sem("var2_ready")
        squared1, log1, rstd1_ready = sem("squared1"), sem("log1"), sem("rstd1_ready")
        squared2, log2, rstd2_ready = sem("squared2"), sem("log2"), sem("rstd2_ready")
        h1_ready = sem("h1_ready")
        part0, resid, part1, part2 = sem("part0"), sem("resid"), sem("part1"), sem("part2")
        v_copied = sem("v_copied")
        biased, maxed, shifted, expd = sem("biased"), sem("maxed"), sem("shifted"), sem("expd")
        prob_copied, divided = sem("prob_copied"), sem("divided")
        den_log, den_ready = sem("den_log"), sem("den_ready")
        x1_ready, h2_ready = sem("x1_ready"), sem("h2_ready")
        parts_out = [[sem(f"parts_out_{n}{i}") for n in "qk"] for i in range(2)]
        stacks_in = [sem(f"stacks_in{i}") for i in range(2)]
        hidden_ready, gelu_ready, down_ready, y_ready = sem("hidden_ready"), sem("gelu_ready"), sem("down_ready"), sem("y_ready")
        stored = [sem("stored0"), sem("stored1")]

        block = ctx.enter_context(nc.Block())

        Q_LAG, S_LAG, T_LAG, P_LAG = 1, 2, 3, 4

        def steps(eng, step, set_up={}):
            def chunks(jt, u):
                c = [(jt + (u - lag) // 2, (u - lag) % 2) for lag in range(P_LAG + 1)]
                return [i if not isinstance(jt, int) or 0 <= 2 * i[0] + i[1] < NCH else None for i in c]

            full0 = P_LAG + P_LAG % 2
            for t in range(full0):
                step(*chunks(t // 2, t % 2))
                if t in set_up:
                    set_up[t]()
            with eng.Fori(full0 // 2, NCH // 2) as jt:
                for u in range(2):
                    step(*chunks(jt, u))
            for t in range(NCH, NCH + P_LAG):
                step(*chunks(t // 2, t % 2))

        def done(c, per, k):
            j, u = c
            return j * (2 * per) + (u * per + k)

        def first(c, n):
            j, u = c
            return isinstance(j, int) and 2 * j + u < n

        def last(c):
            j, u = c
            return isinstance(j, int) and 2 * j + u == NCH - 1

        def cols(buf, c):
            j, u = c
            if isinstance(j, int):
                return buf[:, j, u, :]
            return buf[:, bass.ds(j, 1), u, :].rearrange("p o n -> p (o n)")

        @block.sync
        def _(sp):
            def load_x(c):
                for a in range(2):
                    sp.dma_start(x_sb[2 * C * a:2 * C * (a + 1), 0, c, :],
                                 x_v[0, c, a].rearrange("v c n -> v c n")).then_inc(x_in[c], 16)

            def load_run(y, r0):
                for a in range(2):
                    for v in range(2):
                        g = 2 * a + v
                        sp.dma_start(x_sb[C * g:C * (g + 1), (y * NR + r0) // 2:(y + 1) * NR // 2, :, :],
                                     x_v[y, r0:, a, v, :, :].rearrange("r c n -> c r n")).then_inc(x_in[2 + y], 16)

            load_x(0)
            def load_vector(row, vector, sem):
                n = vector.shape[0] // C
                sp.dma_start(vec_r[row:row + n, :, :], bass.AP(vector.tensor, vector.offset, [[C, n], [0, G], [1, C]]))\
                  .then_inc(sem, 16)

            sp.dma_start(w_rep[:, :, :], qkv_w.unsqueeze(1).to_broadcast([3 * C, G, C])).then_inc(w_in, 16)
            for row, vector in ((0, ln1_g), (1, ln1_b), (2, qkv_b)):
                load_vector(row, vector, w_in)
            load_x(1)
            sp.dma_start(p_nat[:, :], proj_w.unsqueeze(0).to_broadcast([G, C, C])).then_inc(late_in, 16)
            sp.dma_start(f1_rep[:, :, :], fc1_w.unsqueeze(1).to_broadcast([HID, G, C])).then_inc(late_in, 16)
            sp.dma_start(f2_nat[:, :], fc2_w).then_inc(late_in, 16)
            for row, vector in ((5, proj_b), (6, ln2_g), (7, ln2_b), (8, fc2_b)):
                load_vector(row, vector, late_in)
            sp.dma_start(fc1_bc[:, :], fc1_b.rearrange("(p o) -> p o", o=1)).then_inc(late_in, 16)
            load_run(0, 2)
            load_run(1, 0)

            def restack(f, c, s, b, p):
                if c is None:
                    return
                for i in range(2):
                    for n, made in enumerate((part0, part1, part2)):
                        sp.wait_ge(made, done(c, 2, i + 1))
                        sp.dma_start(parts_dram[c[1]][i][n].rearrange("c g n -> g c n"),
                                     parts[:, c[1], i, n, :]).then_inc(parts_out[c[1]][i], 16)
                if first(c, 2):
                    sp.wait_ge(cleared, c[1] + 1)
                for i in range(2):
                    sp.wait_ge(parts_out[c[1]][i], c[0] * 48 + 48)
                    for hh in range(2):
                        for t, n, qi, ki in RUNS:
                            rows = slice(HR * hh + HD * t, HR * hh + HD * (t + n))
                            if i == 0:
                                dst = q_st[rows, c[1], :, hh, :]
                                src = parts_dram[c[1]][0][qi:qi + n, HD * hh:HD * (hh + 1), :, :]\
                                    .rearrange("s c g n -> s c (g n)")
                            else:
                                dst = k_st[rows, c[1], :, :]
                                src = parts_dram[c[1]][1][ki, HD * hh:HD * (hh + 1), :, :]\
                                    .rearrange("c g n -> c (g n)").unsqueeze(0).to_broadcast([n, HD, GP * TC])
                            sp.dma_start(dst, src).then_inc(stacks_in[c[1]], 16)

            steps(sp, restack)

            for c in range(NCH):
                sp.wait_ge(y_ready, c + 1)
                for a in range(2):
                    for v in range(2):
                        g = 2 * a + v
                        sp.dma_start(out_v[c // NR, c % NR, a, v, :, :], y_sb[C * g:C * (g + 1), c % 2, :])\
                          .then_inc(stored[c % 2], 16)
            for u in range(2):
                sp.wait_ge(stored[u], 16 * G * NCH // 2)

        @block.gpsimd
        def _(pool):
            pool.memset(ident[:, :], 0.0).then_inc(ident_ready, 1)
            pool.wait_ge(ident_ready, 1)
            pool.affine_select(out=ident[:, :], in_=ident[:, :], compare_op=ALU.not_equal, fill=1.0,
                               base=0, pattern=[[-1, 128]], channel_multiplier=1).then_inc(ident_ready, 1)
            pool.memset(raw_t[:, :, :], 0.0).then_inc(blank, 1)
            pool.memset(nat[:, :, :], 0.0)
            pool.memset(f1_st[:, :, :], 0.0).then_inc(blank, 1)
            pool.memset(q_st[:, 0, :, :, :].rearrange("p g h n -> p (g h n)").bitcast(fp32), 0.0).then_inc(cleared, 1)
            pool.memset(v_blk[:, :, :, :, :], 0.0).then_inc(blank, 1)
            pool.memset(q_st[:, 1, :, :, :].rearrange("p g h n -> p (g h n)").bitcast(fp32), 0.0).then_inc(cleared, 1)
            for ny in range(WS):
                pool.dma_start(raw_b[WS * ny:WS * (ny + 1), :, :],
                               bass.AP(rpb.tensor, rpb.offset + ny * SIDE * NH,
                                       [[NH, WS], [SIDE * NH, WS], [1, WS * NH]])).then_inc(bias_in, 16)

            def subtract_max(s, k):
                if s is None:
                    return
                pool.wait_ge(maxed, done(s, GP, k + 1))
                tile = prob[:, s[1], k // 2, :, k % 2, :]
                pool.tensor_tensor(tile, tile, mx[:, k % 2, :].unsqueeze(2).to_broadcast([128, NW, NT]),
                                   ALU.subtract).then_inc(shifted, 1)

            def third(a, i):
                if a is None:
                    return
                pool.wait_ge(part1, done(a, 2, i + 1))
                pool.tensor_tensor(parts[:, a[1], i, 2, :], rest[:, i, :], parts[:, a[1], i, 1, :],
                                   ALU.subtract).then_inc(part2, 1)

            def step(f, a, s, b, p):
                third(a, 0)
                third(a, 1)
                subtract_max(s, 0)
                subtract_max(s, 1)
                subtract_max(s, 2)
                subtract_max(s, 3)
                subtract_max(s, 4)
                subtract_max(s, 5)
                subtract_max(s, 6)
                subtract_max(s, 7)

            steps(pool, step)

        @block.scalar
        def _(act):
            act.preload_act_table_set("natural_log_exp_and_others")

            def exp_tile(s, k):
                if s is None:
                    return
                act.wait_ge(shifted, done(s, GP, k + 1))
                tile = prob[:, s[1], k // 2, :, k % 2, :]
                act.activation(tile, tile, ACT.Exp).then_inc(expd, 1)

            def copy_bank(b, k):
                if b is None:
                    return
                act.wait_ge(transposed, done(b, 8, k + 1))
                if k % 4 == 0 and not first(b, 1):
                    act.wait_ge(summed, done(b, 2, k // 4 + 1) - 2)
                act.activation(prob_t[:, k // 4, k % 4, :, :], T_PS[k % 2].rearrange("p (w n) -> p w n", n=128),
                               ACT.Copy).then_inc(prob_copied, 1)

            def log_den(c, half):
                if c is None:
                    return
                act.wait_ge(summed, done(c, 2, half + 1))
                if not (first(c, 1) and half == 0):
                    act.wait_ge(divided, done(c, 2, half))
                act.activation(den[:, :, :, :], D_PS.rearrange("p (w h n) -> p w h n", h=2, n=NT), ACT.Ln)\
                   .then_inc(den_log, 1)

            def exp_den(c, half):
                if c is None:
                    return
                act.wait_ge(den_log, done(c, 2, half + 1))
                act.activation(den[:, :, :, :], den[:, :, :, :], ACT.Exp, scale=-1.0).then_inc(den_ready, 1)

            def first_part(a, i):
                if a is None:
                    return
                bank, made = ((FA, q_ready), (FB, k_ready))[i]
                act.wait_ge(made, done(a, 1, 1))
                if not first(a, 2):
                    act.wait_ge(parts_out[a[1]][i], a[0] * 48)
                act.activation(parts[:, a[1], i, 0, :], bank, ACT.Identity, bias=bq[:, i:i + 1])\
                   .then_inc(part0, 1)

            def copy_v(s):
                if s is None:
                    return
                act.wait_ge(v_ready, done(s, 1, 1))
                if first(s, 1):
                    act.wait_ge(blank, 3)
                if not first(s, 2):
                    act.wait_ge(attended, done(s, 2, 0) - 2)
                for v in range(2):
                    rows = slice(NT * v, NT * (v + 1))
                    ins = act.activation(v_blk[rows, s[1], :, :, HC * v:HC * (v + 1)],
                                         FB[rows].rearrange("p (w q e) -> p w q e", w=NW, q=XP), ACT.Copy)
                ins.then_inc(v_copied, 1)

            def square1(f):
                if f is None:
                    return
                act.wait_ge(centered1, done(f, 1, 1))
                if not first(f, 1):
                    act.wait_ge(var1_ready, done(f, 1, 0))
                act.activation(sq1[:, :], FA, ACT.Square).then_inc(squared1, 1)

            def square2(p):
                if p is None:
                    return
                act.wait_ge(centered2, done(p, 1, 1))
                if not first(p, 1):
                    act.wait_ge(var2_ready, done(p, 1, 0))
                act.activation(sq2[:, :], D_PS, ACT.Square).then_inc(squared2, 1)

            def log_var1(f):
                if f is None:
                    return
                act.wait_ge(var1_ready, done(f, 1, 1))
                if not first(f, 1):
                    act.wait_ge(h1_ready, done(f, 1, 0))
                act.activation(rstd1[:, :], FB, ACT.Ln, bias=eps[:, :]).then_inc(log1, 1)

            def exp_var1(f):
                if f is None:
                    return
                act.wait_ge(log1, done(f, 1, 1))
                act.activation(rstd1[:, :], rstd1[:, :], ACT.Exp, scale=-0.5).then_inc(rstd1_ready, 1)

            def log_var2(p):
                if p is None:
                    return
                act.wait_ge(var2_ready, done(p, 1, 1))
                if not first(p, 1):
                    act.wait_ge(h2_ready, done(p, 1, 0))
                act.activation(rstd2[:, :], O_PS, ACT.Ln, bias=eps[:, :]).then_inc(log2, 1)

            def exp_var2(p):
                if p is None:
                    return
                act.wait_ge(log2, done(p, 1, 1))
                act.activation(rstd2[:, :], rstd2[:, :], ACT.Exp, scale=-0.5).then_inc(rstd2_ready, 1)

            def step(f, a, s, b, p):
                first_part(a, 0)
                exp_tile(b, 6)
                first_part(a, 1)
                exp_tile(b, 7)
                copy_bank(b, 0)
                copy_bank(b, 1)
                log_den(p, 1)
                exp_den(p, 1)
                copy_bank(b, 2)
                square1(f)
                copy_bank(b, 3)
                exp_tile(s, 0)
                copy_v(s)
                exp_tile(s, 1)
                square2(p)
                exp_tile(s, 2)
                copy_bank(b, 4)
                log_var1(f)
                log_var2(p)
                exp_var2(p)
                exp_var1(f)
                copy_bank(b, 5)
                copy_bank(b, 6)
                exp_tile(s, 3)
                log_den(b, 0)
                exp_den(b, 0)
                copy_bank(b, 7)
                exp_tile(s, 4)
                exp_tile(s, 5)

            act.wait_ge(const_ready, 1)
            steps(act, step, {0: lambda: act.wait_ge(weights_ready, 1)})

            def gelu(i2, u):
                for g in range(G):
                    act.wait_ge(hidden_ready, (i2 * 2 + u) * G + g + 1)
                    if not (isinstance(i2, int) and i2 == 0):
                        act.wait_ge(down_ready, (i2 * 2 + (u - 1)) * G + (g + 1 - G))
                    act.activation(hid[:, u, g, :], ps[:, g, :], ACT.Gelu, bias=fb1[:, :]).then_inc(gelu_ready, 1)

            gelu(0, 0)
            gelu(0, 1)
            with act.Fori(1, NCH // 2) as i2:
                gelu(i2, 0)
                gelu(i2, 1)

        @block.vector
        def _(dve):
            n_setup = [0]

            def link(ins):
                n_setup[0] += 1
                ins.then_inc(setup_v, 1)
                dve.wait_ge(setup_v, n_setup[0])

            dve.memset(eps[:, :], 1e-5)
            dve.memset(ones_v[:, :], 0.0)
            link(dve.memset(mean_m[:, :], 0.0))
            for g in range(G):
                dve.memset(mean_m[C * g:C * (g + 1), C * g:C * (g + 1)], 1.0 / C)
            for v in range(2):
                ins = dve.memset(ones_v[64 * v:64 * (v + 1), HC * v:HC * (v + 1)], 1.0)
            link(ins)
            dve.wait_ge(ident_ready, 2)
            dve.tensor_tensor(cent_m[:, :], ident[:, :], mean_m[:, :], ALU.subtract).then_inc(const_ready, 1)
            def set_up_qkv():
                dve.wait_ge(setup_t, 1)
                dve.wait_ge(blank, 1)
                dve.tensor_copy(vec[:, 0:5], ps[:, 0, 0:5])
                for g in range(G):
                    r = slice(C * g, C * (g + 1))
                    ins = dve.tensor_copy(raw_t[r, 0:3, r], ps[r, 1, 0:3 * C].rearrange("p (s o) -> p s o", s=3))
                link(ins)
                dve.tensor_scalar(wqk[:, 0, :], raw_t[:, 0, :], vec[:, 0:1], HD ** -0.5, ALU.mult, ALU.mult)
                dve.tensor_scalar(wqk[:, 1, :], raw_t[:, 1, :], vec[:, 0:1], None, ALU.mult).then_inc(setup_b, 1)
                dve.tensor_scalar(wv[:, :, :, :].rearrange("p v x e -> p x v e"),
                                  raw_t[:, 2, :].rearrange("p (x v e) -> p x v e", x=2, v=2), vec[:, 0:1], None,
                                  ALU.mult)
                dve.wait_ge(setup_t, 2)
                dve.tensor_scalar(bq[:, 0:1], ps[:, 7, 0:1], vec[:, 2:3], HD ** -0.5, ALU.add, ALU.mult)
                dve.tensor_scalar(bq[:, 1:2], ps[:, 7, 1:2], vec[:, 3:4], None, ALU.add)
                dve.tensor_scalar(bq[:, 2:3], ps[:, 7, 2:3], vec[:, 4:5], None, ALU.add).then_inc(weights_ready, 1)
                dve.wait_ge(weights_ready, 1)

            def set_up_rest():
                dve.wait_ge(late_in, 16 * 8)
                dve.wait_ge(blank, 2)
                for a in range(2):
                    for v in range(2):
                        r = slice(C * (2 * a + v), C * (2 * a + v + 1))
                        dve.tensor_copy(nat[r, 0, r], p_nat[r, :])
                        for hh in range(2):
                            dst = nat[r, 1 + hh, :].rearrange("p (x q v e) -> p x q v e", x=2, q=2, v=2)
                            src = p_nat[r, :].rearrange("p (q e) -> p q e", q=2)
                            ins = dve.tensor_copy(dst[:, a, :, v, HD * hh:HD * (hh + 1)],
                                                  src[:, :, HD * hh:HD * (hh + 1)])
                ins.then_inc(nat_ready, 1)
                dve.wait_ge(setup_t, 3)
                dve.tensor_copy(vec[:, 5:9], ps[:, 0, 5:9])
                dve.tensor_copy(raw_t[:, 3, :], ps[:, 2, 0:128])
                dve.tensor_copy(f1_t[:, :], ps[:, 3, 0:HID])
                dve.tensor_copy(wp[:, :, :], ps[:, 2, 128:384].rearrange("p (h o) -> p h o", h=2))
                dve.tensor_copy(f2_st[:, :], ps[:, 3, HID:HID + C]).then_inc(setup_b, 1)
                dve.wait_ge(setup_b, 2)
                for g in range(G):
                    r = slice(C * g, C * (g + 1))
                    dve.tensor_scalar(f1_st[r, g, :], f1_t[r, :], vec[r, 6:7], None, ALU.mult)
                dve.wait_ge(setup_t, 4)
                dve.tensor_scalar(fb1[:, :], ps[:, 7, 3:4], fc1_bc[:, :], None, ALU.add)
                dve.tensor_scalar(bq[:, 3:4], ps[:, 6, 0:1], vec[:, 5:6], None, ALU.add).then_inc(weights_ready, 1)
                dve.wait_ge(weights_ready, 2)

            def make_table():
                dve.wait_ge(bias_in, 16 * WS)
                table = raw_b[:, :, :].rearrange("p y (x h) -> p y x h", h=NH)
                for hh in range(2):
                    for pr in range(2):
                        ins = dve.tensor_copy(bias_t[NT * hh:NT * (hh + 1), pr, :, :], table[:, ::-1, ::-1, 2 * pr + hh])
                ins.then_inc(table_ready, 1)
                dve.wait_ge(table_ready, 1)

            bias_pair = bias_t[:, :, :, :].rearrange("p q y x -> p q (y x)")

            def divide(c, half):
                if c is None:
                    return
                dve.wait_ge(attended, done(c, 2, half + 1))
                dve.wait_ge(den_ready, done(c, 2, half + 1))
                if half == 0 and not first(c, 1):
                    dve.wait_ge(projected, done(c, 1, 0))
                for hh in range(2):
                    dst = att[:, hh, :].rearrange("p (i w j) -> p w i j", i=WS, j=WS)[:, 4 * half:4 * half + 4]
                    src = O_PS.rearrange("p (w h i j) -> p h w i j", w=4, h=2, i=WS)[:, hh]
                    ins = dve.tensor_tensor(dst, src, den[:, :, hh, :].rearrange("p w (i j) -> p w i j", i=WS),
                                            ALU.mult)
                ins.then_inc(divided, 1)

            def rest_of(a, i):
                if a is None:
                    return
                dve.wait_ge((q_ready, k_ready)[i], done(a, 1, 1))
                dve.wait_ge(part0, done(a, 2, i + 1))
                if not first(a, 1):
                    dve.wait_ge(part2, done(a, 2, i + 1) - 2)
                dve.scalar_tensor_tensor(out=rest[:, i, :], in0=(FA, FB)[i], scalar=bq[:, i:i + 1],
                                         in1=parts[:, a[1], i, 0, :], op0=ALU.add, op1=ALU.subtract)\
                   .then_inc(resid, 1)

            def second_part(a, i):
                if a is None:
                    return
                dve.wait_ge(resid, done(a, 2, i + 1))
                if not first(a, 2):
                    dve.wait_ge(parts_out[a[1]][i], a[0] * 48)
                dve.tensor_copy(parts[:, a[1], i, 1, :], rest[:, i, :]).then_inc(part1, 1)

            def add_bias(s, k):
                if s is None:
                    return
                if first(s, 1) and k == 0:
                    make_table()
                dve.wait_ge(scores_ready, done(s, GP, k + 1))
                if k == 0 and not first(s, 2):
                    dve.wait_ge(transposed, done(s, 8, 0) - 8)
                pair = (k // 2) % 2
                dve.tensor_tensor(prob[:, s[1], k // 2, :, k % 2, :], S_PS[k % 2].rearrange("p (w m) -> p w m", m=NT),
                                  bias_pair[:, pair, :].unsqueeze(1).to_broadcast([128, NW, NT]),
                                  ALU.add).then_inc(biased, 1)

            def find_max(s, k):
                if s is None:
                    return
                dve.wait_ge(biased, done(s, GP, k + 1))
                if not (first(s, 1) and k < 2):
                    dve.wait_ge(shifted, done(s, GP, k + 1) - 2)
                dve.reduce_max(mx[:, k % 2, :], prob[:, s[1], k // 2, :, k % 2, :], AX.X).then_inc(maxed, 1)

            def residual(p):
                if p is None:
                    return
                dve.wait_ge(projected, done(p, 1, 1))
                dve.scalar_tensor_tensor(out=cols(x1_sb, p), in0=O_PS, scalar=bq[:, 3:4],
                                         in1=cols(x_sb, p), op0=ALU.add, op1=ALU.add).then_inc(x1_ready, 1)

            def norm2(p):
                if p is None:
                    return
                dve.wait_ge(rstd2_ready, done(p, 1, 1))
                dve.tensor_tensor(cols(x_sb, p), D_PS, rstd2[:, :], ALU.mult).then_inc(h2_ready, 1)

            def norm1(f):
                if f is None:
                    return
                dve.wait_ge(rstd1_ready, done(f, 1, 1))
                if not first(f, 2):
                    dve.wait_ge(v_ready, done(f, 1, 0) - 1)
                dve.tensor_tensor(h1[:, f[1], :, :].rearrange("p w (i j) -> p w i j", i=WS),
                                  FA.rearrange("p (i w j) -> p w i j", i=WS, j=WS),
                                  rstd1[:, :].rearrange("p (i w j) -> p w i j", i=WS, j=WS),
                                  ALU.mult).then_inc(h1_ready, 1)

            def step(f, a, s, b, p):
                rest_of(a, 0)
                second_part(a, 0)
                add_bias(s, 0)
                rest_of(a, 1)
                add_bias(s, 1)
                second_part(a, 1)
                find_max(s, 0)
                divide(p, 1)
                add_bias(s, 2)
                find_max(s, 1)
                find_max(s, 2)
                add_bias(s, 3)
                residual(p)
                find_max(s, 3)
                add_bias(s, 4)
                find_max(s, 4)
                add_bias(s, 5)
                add_bias(s, 6)
                norm2(p)
                find_max(s, 5)
                norm1(f)
                add_bias(s, 7)
                find_max(s, 6)
                find_max(s, 7)
                divide(b, 0)

            steps(dve, step, {0: set_up_qkv, 1: set_up_rest})

            def finish(i2, u):
                n = i2 * 2 + u
                dve.wait_ge(down_ready, (i2 * 2 + u) * G + G)
                if not (isinstance(i2, int) and i2 == 0):
                    dve.wait_ge(stored[u], i2 * (16 * G))
                dve.scalar_tensor_tensor(out=y_sb[:, u, :], in0=ps[:, 4 + u, :], scalar=vec[:, 8:9],
                                         in1=cols(x1_sb, (i2, u)), op0=ALU.add, op1=ALU.add).then_inc(y_ready, 1)

            finish(0, 0)
            finish(0, 1)
            with dve.Fori(1, NCH // 2) as i2:
                finish(i2, 0)
                finish(i2, 1)

        @block.tensor
        def _(pe):
            def set_up_qkv():
                pe.wait_ge(w_in, 16 * 4)
                pe.transpose(ps[:, 0, 0:5], vec_r[0:5, :, :].rearrange("p g c -> p (g c)"), ident[0:5, 0:5])
                pe.transpose(ps[:, 1, 0:3 * C], w_rep[:, :, :].rearrange("p g c -> p (g c)"), ident[0:3 * C, 0:3 * C])\
                  .then_inc(setup_t, 1)
                pe.wait_ge(setup_b, 1)
                for i in range(3):
                    ins = pe.matmul(ps[:, 7, i:i + 1], raw_t[:, i, :], vec[:, 1:2], start=True, stop=True)
                ins.then_inc(setup_t, 1)

            def set_up_rest():
                pe.wait_ge(late_in, 16 * 8)
                pe.transpose(ps[:, 0, 0:9], vec_r[:, :, :].rearrange("p g c -> p (g c)"), ident[0:9, 0:9])
                pe.transpose(ps[:, 3, 0:HID], f1_rep[:, :, :].rearrange("p g c -> p (g c)"), ident[:, :])
                pe.transpose(ps[:, 3, HID:HID + C], f2_nat[:, :], ident[0:C, 0:C])
                pe.wait_ge(nat_ready, 1)
                for i in range(3):
                    ins = pe.transpose(ps[:, 2, 128 * i:128 * (i + 1)], nat[:, i, :], ident[:, :])
                ins.then_inc(setup_t, 1)
                pe.wait_ge(setup_b, 2)
                pe.wait_ge(weights_ready, 1)
                pe.matmul(ps[:, 7, 3:4], f1_t[0:C, :], vec[0:C, 7:8], start=True, stop=True)
                pe.matmul(ps[:, 6, 0:1], raw_t[:, 3, :], bq[:, 2:3], start=True, stop=True).then_inc(setup_t, 1)

            def attend(c, half):
                if c is None:
                    return
                pe.wait_ge(prob_copied, done(c, 8, 4 * half + 4))
                pe.wait_ge(v_copied, done(c, 1, 1))
                if half == 1:
                    pe.wait_ge(divided, done(c, 2, 1))
                elif not first(c, 1):
                    pe.wait_ge(log2, done(c, 1, 0))
                for w in range(4):
                    for q in range(XP):
                        ins = pe.matmul(O_PS[32 * q:32 * (q + 1), 128 * w:128 * (w + 1)],
                                        v_blk[:, c[1], 4 * half + w, q, :], prob_t[:, half, q, w, :],
                                        start=True, stop=True, tile_position=(0, 32 * q))
                ins.then_inc(attended, 1)

            def sum_keys(c, half):
                if c is None:
                    return
                if half == 0 and not first(c, 1):
                    pe.wait_ge(h2_ready, done(c, 1, 0))
                if half == 1:
                    pe.wait_ge(den_log, done(c, 2, 1))
                for q in range(XP):
                    ins = pe.matmul(D_PS[32 * q:32 * (q + 1), :], ones_v[:, :],
                                    prob_t[:, half, q, :, :].rearrange("p w n -> p (w n)"),
                                    start=True, stop=True, tile_position=(0, 32 * q))
                ins.then_inc(summed, 1)

            def make_qk(a):
                if a is None:
                    return
                pe.wait_ge(h1_ready, done(a, 1, 1))
                pe.matmul(FA, wqk[:, 0, :], h1[:, a[1], :, :].rearrange("p w n -> p n w"),
                          start=True, stop=True).then_inc(q_ready, 1)
                pe.matmul(FB, wqk[:, 1, :], h1[:, a[1], :, :].rearrange("p w n -> p (w n)"),
                          start=True, stop=True).then_inc(k_ready, 1)

            def score(s, k):
                if s is None:
                    return
                gp = (2 * (k // 4) + k % 2) * 2 + (k // 2) % 2
                if k == 0:
                    pe.wait_ge(stacks_in[s[1]], s[0] * (16 * READS) + 16 * READS)
                if not (first(s, 1) and k < 2):
                    pe.wait_ge(biased, done(s, GP, k + 1) - 2)
                q_w = q_st[:, s[1], gp, :, :].rearrange("p h n -> p (h n)").rearrange("p (m w) -> p w m", w=NW)
                for w in range(NW):
                    ins = pe.matmul(S_PS[k % 2][:, NT * w:NT * (w + 1)], q_w[:, w, :],
                                    k_st[:, s[1], gp, NT * w:NT * (w + 1)], start=True, stop=True)
                ins.then_inc(scores_ready, 1)

            def turn(b, k):
                if b is None:
                    return
                half, q = k // 4, k % 4
                if half == 0:
                    pe.wait_ge(expd, done(b, GP, 2 * q + 2))
                if not (first(b, 1) and k < 2):
                    pe.wait_ge(prob_copied, done(b, 8, k + 1) - 2)
                for w in range(4):
                    ins = pe.transpose(T_PS[k % 2][:, 128 * w:128 * (w + 1)],
                                       prob[:, b[1], q, 4 * half + w, :, :].rearrange("p v m -> p (v m)"),
                                       ident[:, :])
                ins.then_inc(transposed, 1)

            def project(p):
                if p is None:
                    return
                pe.wait_ge(divided, done(p, 2, 2))
                for hh in range(2):
                    ins = pe.matmul(O_PS, wp[:, hh, :], att[:, hh, :], start=(hh == 0), stop=(hh == 1))
                ins.then_inc(projected, 1)

            def center1(f, a):
                if f is None:
                    return
                for t, (i, loads) in enumerate(((0, 2), (1, 2), (2, G), (3, G))):
                    if first(f, t + 1) and not first(f, t):
                        pe.wait_ge(x_in[i], 16 * loads)
                if a is not None:
                    pe.wait_ge(resid, done(a, 2, 1))
                pe.matmul(FA, cent_m[:, :], cols(x_sb, f), start=True, stop=True).then_inc(centered1, 1)

            def make_v(s, a):
                if s is None:
                    return
                if a is not None:
                    pe.wait_ge(resid, done(a, 2, 2))
                else:
                    pe.wait_ge(v_copied, done(s, 1, 0))
                for w in range(NW):
                    for v in range(2):
                        ins = pe.matmul(FB[64 * v:64 * (v + 1), 64 * w:64 * (w + 1)], h1[:, s[1], w, :],
                                        wv[:, v, :, :].rearrange("p x e -> p (x e)"), start=True, stop=True,
                                        tile_position=(0, 64 * v))
                ins.then_inc(v_ready, 1)

            def variance1(f, a, s):
                if f is None:
                    return
                pe.wait_ge(squared1, done(f, 1, 1))
                if s is not None:
                    pe.wait_ge(v_copied, done(s, 1, 1))
                elif a is not None:
                    pe.wait_ge(resid, done(a, 2, 2))
                pe.matmul(FB, mean_m[:, :], sq1[:, :], start=True, stop=True).then_inc(var1_ready, 1)

            def center2(p):
                if p is None:
                    return
                pe.wait_ge(x1_ready, done(p, 1, 1))
                pe.matmul(D_PS, cent_m[:, :], cols(x1_sb, p), start=True, stop=True).then_inc(centered2, 1)

            def variance2(p):
                if p is None:
                    return
                pe.wait_ge(squared2, done(p, 1, 1))
                pe.matmul(O_PS, mean_m[:, :], sq2[:, :], start=True, stop=True).then_inc(var2_ready, 1)

            def step(f, a, s, b, p):
                turn(b, 0)
                make_qk(a)
                turn(b, 1)
                attend(p, 1)
                score(s, 0)
                sum_keys(p, 1)
                score(s, 1)
                center1(f, a)
                score(s, 2)
                turn(b, 2)
                turn(b, 3)
                make_v(s, a)
                score(s, 3)
                project(p)
                score(s, 4)
                turn(b, 4)
                score(s, 5)
                center2(p)
                variance1(f, a, s)
                variance2(p)
                score(s, 6)
                turn(b, 5)
                turn(b, 6)
                score(s, 7)
                attend(b, 0)
                sum_keys(b, 0)
                turn(b, 7)

            pe.wait_ge(const_ready, 1)
            steps(pe, step, {0: set_up_qkv, 1: set_up_rest})

            pe.wait_ge(h2_ready, NCH)
            pe.wait_ge(log2, NCH)
            pe.wait_ge(prob_copied, 8 * NCH)

            def up(i2, u, g):
                if not (isinstance(i2, int) and 2 * i2 + u == 0):
                    pe.wait_ge(gelu_ready, (i2 * 2 + u) * G + (g + 1 - G))
                pe.matmul(ps[:, g, :], f1_st[:, g, :], cols(x_sb, (i2, u)), start=True, stop=True)\
                  .then_inc(hidden_ready, 1)

            def down(i2, u, g):
                if g == 0 and not (isinstance(i2, int) and i2 == 0):
                    pe.wait_ge(y_ready, i2 * 2 + (u - 1))
                pe.wait_ge(gelu_ready, (i2 * 2 + u) * G + g + 1)
                pe.matmul(ps[C * g:C * (g + 1), 4 + u, :], f2_st[:, :], hid[:, u, g, :], start=True, stop=True,
                          tile_position=(0, C * g)).then_inc(down_ready, 1)

            for g in range(G):
                up(0, 0, g)
            for g in range(G):
                up(0, 1, g)
                down(0, 0, g)
            with pe.Fori(1, NCH // 2) as i2:
                for g in range(G):
                    up(i2, 0, g)
                    down(i2 - 1, 1, g)
                for g in range(G):
                    up(i2, 1, g)
                    down(i2, 0, g)
            for g in range(G):
                down(NCH // 2 - 1, 1, g)


_INS = ['x', 'L0_conv_ln1_g', 'L0_conv_ln1_b', 'L0_conv_qkv_w', 'L0_conv_qkv_b', 'L0_conv_rpb', 'L0_conv_proj_w',
        'L0_conv_proj_b', 'L0_conv_ln2_g', 'L0_conv_ln2_b', 'L0_conv_fc1_w', 'L0_conv_fc1_b', 'L0_conv_fc2_w',
        'L0_conv_fc2_b']


def kernel(**inputs):
    import numpy as _np
    import concourse.bacc as _bacc
    from concourse import mybir as _mybir
    from concourse.bass_utils import run_bass_kernel_spmd as _run

    nc = _bacc.Bacc("TRN2", target_bir_lowering=False, num_devices=1)
    arrays, args = {}, []
    for name in _INS:
        a = _np.ascontiguousarray(inputs[name])
        arrays[f"in_{name}_dram"] = a
        args.append(nc.dram_tensor(f"in_{name}_dram", a.shape, _mybir.dt.from_np(a.dtype), kind="ExternalInput").ap())
    shape = _np.shape(inputs['x'])
    args.append(nc.dram_tensor("out_0_dram", shape, _mybir.dt.float32, kind="ExternalOutput").ap())
    swin_block_kernel(nc, *args)
    r = _run(nc, [arrays], core_ids=[0])
    return r.results[0]["out_0_dram"]
```

```python
from contextlib import ExitStack

import concourse.bass as bass
from concourse import mybir


def swin_block_kernel(nc, x, ln1_g, ln1_b, qkv_w, qkv_b, rpb, proj_w, proj_b,
                      ln2_g, ln2_b, fc1_w, fc1_b, fc2_w, fc2_b, out):
    fp32, bf16 = mybir.dt.float32, mybir.dt.bfloat16
    ALU, ACT, AX = mybir.AluOpType, mybir.ActivationFunctionType, mybir.AxisListType

    B, C, H, W = x.shape
    WS = 8
    NT = WS * WS
    NH = rpb.shape[1]
    HD = C // NH
    G = 128 // C
    NW = W // WS
    TC = WS * W
    HC = C // 2
    NCH = B * H * W // (G * TC)
    NR = NCH // 2
    HID = fc1_w.shape[0]
    SIDE = 2 * WS - 1
    TERMS = [(0, 0), (1, 0), (2, 0), (0, 1), (1, 1), (0, 2)]
    RUNS = [(0, 3, 0, 0), (3, 2, 0, 1), (5, 1, 0, 2)]
    HR = len(TERMS) * HD
    KR = 2 * HR
    GP = 2 * G
    XP = 4
    READS = 2 * 2 * len(RUNS)

    x_v = x.rearrange("(a y) c (r v i) w -> y r a v c (i w)", y=2, v=2, i=WS)
    out_v = out.rearrange("(a y) c (r v i) w -> y r a v c (i w)", y=2, v=2, i=WS)

    ctx = ExitStack()
    with ctx:
        def sb(name, shape, dt=fp32):
            return ctx.enter_context(nc.sbuf_tensor(name, shape, dt))

        def sem(name):
            return ctx.enter_context(nc.semaphore(name))

        parts_dram = [[nc.dram_tensor(f"parts_{n}{i}", [3, HC, GP, TC], bf16).ap() for n in "qk"] for i in range(2)]
        h2_dram = nc.dram_tensor("h2_parts", [NCH // 2, 2, 3, C, G, TC], bf16).ap()

        x_sb = sb("x_sb", [128, NCH // 2, 2, TC])
        x1_sb = sb("x1_sb", [128, NCH // 2, 2, TC])
        sq1 = sb("sq1", [128, TC])
        rstd1 = sb("rstd1", [128, TC])
        sq2 = sb("sq2", [128, TC])
        rstd2 = sb("rstd2", [128, TC])
        h1 = sb("h1", [128, 2, NW, NT])
        rest = sb("rest", [128, 2, TC])
        parts = sb("parts", [128, 2, 2, 3, TC], bf16)
        q_st = sb("q_st", [128, 2, GP, 2, TC], bf16)
        k_st = sb("k_st", [KR, 2, GP, TC], bf16)
        prob = sb("prob", [128, 2, XP, NW, 2, NT])
        prob_t = sb("prob_t", [128, 2, XP, 4, 128])
        v_blk = sb("v_blk", [128, 2, NW, XP, 2 * HC])
        den = sb("den", [128, 4, 2, NT])
        att = sb("att", [128, 2, TC])

        ident = sb("ident", [128, 128])
        mean_m = sb("mean_m", [128, 128])
        cent_m = sb("cent_m", [128, 128])
        ones_v = sb("ones_v", [128, 2 * HC])
        eps = sb("eps", [128, 1])
        mx = sb("mx", [128, 2, NW])
        raw_b = sb("raw_b", [NT, WS, WS * NH])
        bias_t = sb("bias_t", [128, 2, WS, WS])
        vec_r = sb("vec_r", [9, G, C])
        vec = sb("vec", [128, 9])
        fc1_bc = sb("fc1_bc", [HID, 1])
        p_nat = sb("p_nat", [128, C])
        f2_nat = sb("f2_nat", [C, HID])
        w_rep = sb("w_rep", [3 * C, G, C])
        f1_rep = sb("f1_rep", [HID, G, C])
        nat = sb("nat", [128, 3, 128])
        raw_t = sb("raw_t", [128, 4, 128])
        wqk = sb("wqk", [128, 2, 128])
        wv = sb("wv", [128, 2, 2, C])
        wp = sb("wp", [128, 2, 128])
        f1_t = sb("f1_t", [128, HID])
        f1_s = sb("f1_s", [128, 2, HID])
        f1_p = sb("f1_p", [128, 3, HID], bf16)
        f1_st = sb("f1_st", [128, 2, HID], bf16)
        f2_st = sb("f2_st", [HID, C])
        bq = sb("bq", [128, 4])
        fb1 = sb("fb1", [HID, 1])
        h2 = sb("h2", [128, TC])
        h2_p = sb("h2_p", [128, 3, TC], bf16)
        h2_st = q_st[:, :, :, :, :].rearrange("p a g h n -> p (a g h n)").rearrange("p (c g n) -> p c g n", g=G, n=TC)
        hid = prob[:, :, 0:2, :, :, :].rearrange("p u q w v m -> p u (q w v m)").rearrange("p u (g n) -> p u g n", g=G)
        y_sb = prob[:, :, 2, 0:4, :, :].rearrange("p u w v m -> p u (w v m)")

        ps = ctx.enter_context(nc.psum_tensor("ps", [128, 8, TC], fp32))
        S_PS = [ps[:, 0, :], ps[:, 1, :]]
        T_PS = [ps[:, 2, :], ps[:, 3, :]]
        FA, FB = ps[:, 4, :], ps[:, 5, :]
        OD_PS = [ps[:, 6, :], ps[:, 7, :]]

        x_in = [sem(f"x_in{i}") for i in range(4)]
        w_in = sem("w_in")
        late_in = sem("late_in")
        bias_in = sem("bias_in")
        cleared = [sem("cleared0"), sem("cleared1")]
        ident_ready = sem("ident_ready")
        const_ready = sem("const_ready")
        blank, blank_v = sem("blank"), sem("blank_v")
        nat_ready = sem("nat_ready")
        setup_t = sem("setup_t")
        setup_v = sem("setup_v")
        setup_b = sem("setup_b")
        weights_ready = sem("weights_ready")
        table_ready = sem("table_ready")
        centered1, var1_ready = sem("centered1"), sem("var1_ready")
        q_ready, k_ready, v_ready = sem("q_ready"), sem("k_ready"), sem("v_ready")
        scores_ready, transposed = sem("scores_ready"), sem("transposed")
        attended, summed = sem("attended"), sem("summed")
        projected, centered2, var2_ready = sem("projected"), sem("centered2"), sem("var2_ready")
        squared1, log1, rstd1_ready = sem("squared1"), sem("log1"), sem("rstd1_ready")
        squared2, log2, rstd2_ready = sem("squared2"), sem("log2"), sem("rstd2_ready")
        h1_ready = sem("h1_ready")
        part0, resid, part1, part2 = sem("part0"), sem("resid"), sem("part1"), sem("part2")
        v_copied = sem("v_copied")
        biased, maxed, shifted, expd = sem("biased"), sem("maxed"), sem("shifted"), sem("expd")
        prob_copied, divided = sem("prob_copied"), sem("divided")
        den_log, den_ready = sem("den_log"), sem("den_ready")
        x1_ready, h2_ready = sem("x1_ready"), sem("h2_ready")
        h2_part0, h2_rest, h2_part1, h2_part2 = sem("h2_part0"), sem("h2_rest"), sem("h2_part1"), sem("h2_part2")
        h2_out = sem("h2_out")
        h2_in = [sem(f"h2_in{i}") for i in range(3)]
        parts_out = [[sem(f"parts_out_{n}{i}") for n in "qk"] for i in range(2)]
        stacks_in = [sem(f"stacks_in{i}") for i in range(2)]
        hidden_ready, gelu_ready, down_ready, y_ready = sem("hidden_ready"), sem("gelu_ready"), sem("down_ready"), sem("y_ready")
        stored = [sem("stored0"), sem("stored1")]

        block = ctx.enter_context(nc.Block())

        Q_LAG, S_LAG, T_LAG, P_LAG = 1, 2, 3, 4

        before_last, last = (NCH // 2 - 1, 0), (NCH // 2 - 1, 1)

        def banks(c):
            return (FA, FB) if c is last else OD_PS

        def steps(eng, step, extra={}):
            def chunks(jt, u):
                c = [(jt + (u - lag) // 2, (u - lag) % 2) for lag in range(P_LAG + 1)]
                c = [last if isinstance(jt, int) and i == last else i for i in c]
                return [i if not isinstance(jt, int) or 0 <= 2 * i[0] + i[1] < NCH else None for i in c]

            full0 = P_LAG + P_LAG % 2
            for t in range(full0):
                step(*chunks(t // 2, t % 2))
                if t in extra:
                    extra[t]()
            with eng.Fori(full0 // 2, NCH // 2) as jt:
                for u in range(2):
                    step(*chunks(jt, u))
            for t in range(NCH, NCH + P_LAG - 2):
                step(*chunks(t // 2, t % 2))
                if t in extra:
                    extra[t]()

        def done(c, per, k):
            j, u = c
            return j * (2 * per) + (u * per + k)

        def first(c, n):
            j, u = c
            return isinstance(j, int) and 2 * j + u < n

        def cols(buf, c):
            j, u = c
            if isinstance(j, int):
                return buf[:, j, u, :]
            return buf[:, bass.ds(j, 1), u, :].rearrange("p o n -> p (o n)")

        @block.sync
        def _(sp):
            def load_x(c):
                for a in range(2):
                    sp.dma_start(x_sb[2 * C * a:2 * C * (a + 1), 0, c, :],
                                 x_v[0, c, a].rearrange("v c n -> v c n")).then_inc(x_in[c], 16)

            def load_run(y, r0):
                for a in range(2):
                    for v in range(2):
                        g = 2 * a + v
                        sp.dma_start(x_sb[C * g:C * (g + 1), (y * NR + r0) // 2:(y + 1) * NR // 2, :, :],
                                     x_v[y, r0:, a, v, :, :].rearrange("r c n -> c r n")).then_inc(x_in[2 + y], 16)

            load_x(0)
            def load_vector(row, vector, sem):
                n = vector.shape[0] // C
                sp.dma_start(vec_r[row:row + n, :, :], bass.AP(vector.tensor, vector.offset, [[C, n], [0, G], [1, C]]))\
                  .then_inc(sem, 16)

            sp.dma_start(w_rep[:, :, :], qkv_w.unsqueeze(1).to_broadcast([3 * C, G, C])).then_inc(w_in, 16)
            for row, vector in ((0, ln1_g), (1, ln1_b), (2, qkv_b)):
                load_vector(row, vector, w_in)
            load_x(1)
            sp.dma_start(p_nat[:, :], proj_w.unsqueeze(0).to_broadcast([G, C, C])).then_inc(late_in, 16)
            sp.dma_start(f1_rep[:, :, :], fc1_w.unsqueeze(1).to_broadcast([HID, G, C])).then_inc(late_in, 16)
            sp.dma_start(f2_nat[:, :], fc2_w).then_inc(late_in, 16)
            for row, vector in ((5, proj_b), (6, ln2_g), (7, ln2_b), (8, fc2_b)):
                load_vector(row, vector, late_in)
            sp.dma_start(fc1_bc[:, :], fc1_b.rearrange("(p o) -> p o", o=1)).then_inc(late_in, 16)
            load_run(0, 2)
            load_run(1, 0)

            def restack(c):
                if c is None:
                    return
                for i in range(2):
                    for n, made in enumerate((part0, part1, part2)):
                        sp.wait_ge(made, done(c, 2, i + 1))
                        sp.dma_start(parts_dram[c[1]][i][n].rearrange("c g n -> g c n"),
                                     parts[:, c[1], i, n, :]).then_inc(parts_out[c[1]][i], 16)
                if first(c, 2):
                    sp.wait_ge(cleared[c[1]], 1)
                for i in range(2):
                    sp.wait_ge(parts_out[c[1]][i], c[0] * 48 + 48)
                    for hh in range(2):
                        for t, n, qi, ki in RUNS:
                            rows = slice(HR * hh + HD * t, HR * hh + HD * (t + n))
                            if i == 0:
                                dst = q_st[rows, c[1], :, hh, :]
                                src = parts_dram[c[1]][0][qi:qi + n, HD * hh:HD * (hh + 1), :, :]\
                                    .rearrange("s c g n -> s c (g n)")
                            else:
                                dst = k_st[rows, c[1], :, :]
                                src = parts_dram[c[1]][1][ki, HD * hh:HD * (hh + 1), :, :]\
                                    .rearrange("c g n -> c (g n)").unsqueeze(0).to_broadcast([n, HD, GP * TC])
                            sp.dma_start(dst, src).then_inc(stacks_in[c[1]], 16)

            def store_h2(p):
                if p is None:
                    return
                for n, made in enumerate((h2_part0, h2_part1, h2_part2)):
                    sp.wait_ge(made, done(p, 1, 1))
                    if isinstance(p[0], int):
                        dst = h2_dram[p[0], p[1], n]
                    else:
                        dst = h2_dram[bass.ds(p[0], 1), p[1], n].rearrange("o c g n -> (o c) g n")
                    sp.dma_start(dst.rearrange("c g n -> g c n"), h2_p[:, n, :]).then_inc(h2_out, 16)

            def load_h2(first_c, end_c, loaded):
                sp.wait_ge(scores_ready, GP * NCH)
                sp.wait_ge(h2_out, 48 * end_c)
                for c in range(first_c, end_c):
                    for row, parts_in in ((0, 3), (3, 1)):
                        sp.dma_start(h2_st[C * row:C * (row + parts_in), c, :, :].rearrange("p g n -> p (g n)"),
                                     h2_dram[c // 2, c % 2, 0:parts_in].rearrange("s c g n -> (s c) (g n)"))\
                          .then_inc(loaded, 16)

            def step(f, a, s, b, p):
                restack(a)
                store_h2(p)

            steps(sp, step, {NCH + S_LAG - 1: lambda: load_h2(0, NCH - 2, h2_in[0])})
            store_h2(before_last)
            load_h2(NCH - 2, NCH - 1, h2_in[1])

            for c in range(NCH):
                sp.wait_ge(y_ready, c + 1)
                for a in range(2):
                    sp.dma_start(out_v[c // NR, c % NR, a].rearrange("v c n -> v c n"),
                                 y_sb[2 * C * a:2 * C * (a + 1), c % 2, :]).then_inc(stored[c % 2], 16)
                if c == 0:
                    store_h2(last)
                    load_h2(NCH - 1, NCH, h2_in[2])
            for u in range(2):
                sp.wait_ge(stored[u], 16 * 2 * NCH // 2)

        @block.gpsimd
        def _(pool):
            pool.memset(ident[:, :], 0.0).then_inc(ident_ready, 1)
            pool.wait_ge(ident_ready, 1)
            pool.affine_select(out=ident[:, :], in_=ident[:, :], compare_op=ALU.not_equal, fill=1.0,
                               base=0, pattern=[[-1, 128]], channel_multiplier=1).then_inc(ident_ready, 1)
            pool.memset(raw_t[:, :, :], 0.0).then_inc(blank, 1)
            pool.memset(nat[:, :, :], 0.0)
            pool.memset(f1_st[:, 1, :], 0.0).then_inc(blank, 1)
            pool.memset(q_st[0:KR, 0, :, :, :].rearrange("p g h n -> p (g h n)").bitcast(fp32), 0.0).then_inc(cleared[0], 1)
            for ny in range(WS):
                pool.dma_start(raw_b[WS * ny:WS * (ny + 1), :, :],
                               bass.AP(rpb.tensor, rpb.offset + ny * SIDE * NH,
                                       [[NH, WS], [SIDE * NH, WS], [1, WS * NH]])).then_inc(bias_in, 16)

            def subtract_max(s, k):
                if s is None:
                    return
                pool.wait_ge(maxed, done(s, GP, k + 1))
                tile = prob[:, s[1], k // 2, :, k % 2, :]
                pool.tensor_tensor(tile, tile, mx[:, k % 2, :].unsqueeze(2).to_broadcast([128, NW, NT]),
                                   ALU.subtract).then_inc(shifted, 1)

            def third(a, i):
                if a is None:
                    return
                pool.wait_ge(part1, done(a, 2, i + 1))
                pool.tensor_tensor(parts[:, a[1], i, 2, :], rest[:, i, :], parts[:, a[1], i, 1, :],
                                   ALU.subtract).then_inc(part2, 1)

            def rest_h2(p):
                if p is None:
                    return
                pool.wait_ge(h2_part0, done(p, 1, 1))
                pool.tensor_tensor(h2[:, :], h2[:, :], h2_p[:, 0, :], ALU.subtract).then_inc(h2_rest, 1)

            def third_h2(p):
                if p is None:
                    return
                pool.wait_ge(h2_part1, done(p, 1, 1))
                pool.tensor_tensor(h2_p[:, 2, :], h2[:, :], h2_p[:, 1, :], ALU.subtract).then_inc(h2_part2, 1)

            def step(f, a, s, b, p):
                third(a, 0)
                third(a, 1)
                subtract_max(s, 0)
                subtract_max(s, 1)
                subtract_max(s, 2)
                subtract_max(s, 3)
                subtract_max(s, 4)
                subtract_max(s, 5)
                rest_h2(p)
                subtract_max(s, 6)
                subtract_max(s, 7)
                third_h2(p)

            steps(pool, step)
            p, b = before_last, last
            rest_h2(p)
            third_h2(p)
            rest_h2(last)
            third_h2(last)

        @block.scalar
        def _(act):
            act.preload_act_table_set("natural_log_exp_and_others")

            def exp_tile(s, k):
                if s is None:
                    return
                act.wait_ge(shifted, done(s, GP, k + 1))
                tile = prob[:, s[1], k // 2, :, k % 2, :]
                act.activation(tile, tile, ACT.Exp).then_inc(expd, 1)

            def copy_bank(b, k):
                if b is None:
                    return
                act.wait_ge(transposed, done(b, 8, k + 1))
                if k % 4 == 0 and not first(b, 1):
                    act.wait_ge(summed, done(b, 2, k // 4 + 1) - 2)
                act.activation(prob_t[:, k // 4, k % 4, :, :], T_PS[k % 2].rearrange("p (w n) -> p w n", n=128),
                               ACT.Copy).then_inc(prob_copied, 1)

            def log_den(c, half):
                if c is None:
                    return
                act.wait_ge(summed, done(c, 2, half + 1))
                if not (first(c, 1) and half == 0):
                    act.wait_ge(divided, done(c, 2, half))
                act.activation(den[:, :, :, :], banks(c)[1].rearrange("p (w h n) -> p w h n", h=2, n=NT), ACT.Ln)\
                   .then_inc(den_log, 1)

            def exp_den(c, half):
                if c is None:
                    return
                act.wait_ge(den_log, done(c, 2, half + 1))
                act.activation(den[:, :, :, :], den[:, :, :, :], ACT.Exp, scale=-1.0).then_inc(den_ready, 1)

            def first_part(a, i):
                if a is None:
                    return
                bank, made = ((FA, q_ready), (FB, k_ready))[i]
                act.wait_ge(made, done(a, 1, 1))
                if not first(a, 2):
                    act.wait_ge(parts_out[a[1]][i], a[0] * 48)
                act.activation(parts[:, a[1], i, 0, :], bank, ACT.Identity, bias=bq[:, i:i + 1])\
                   .then_inc(part0, 1)

            def copy_v(s):
                if s is None:
                    return
                act.wait_ge(v_ready, done(s, 1, 1))
                if first(s, 1):
                    act.wait_ge(blank_v, 1)
                if not first(s, 2):
                    act.wait_ge(attended, done(s, 2, 0) - 2)
                for v in range(2):
                    for w in range(2):
                        src = FB[NT * w:NT * (w + 1)].rearrange("p (w v q e) -> p v w q e", v=2, q=XP, e=HC)
                        ins = act.activation(v_blk[NT * v:NT * (v + 1), s[1], w::2, :, HC * v:HC * (v + 1)],
                                             src[:, v, :, :, :], ACT.Copy)
                ins.then_inc(v_copied, 1)

            def square1(f):
                if f is None:
                    return
                act.wait_ge(centered1, done(f, 1, 1))
                if not first(f, 1):
                    act.wait_ge(var1_ready, done(f, 1, 0))
                act.activation(sq1[:, :], FA, ACT.Square).then_inc(squared1, 1)

            def square2(p):
                if p is None:
                    return
                act.wait_ge(centered2, done(p, 1, 1))
                if not first(p, 1):
                    act.wait_ge(var2_ready, done(p, 1, 0))
                act.activation(sq2[:, :], banks(p)[1], ACT.Square).then_inc(squared2, 1)

            def log_var1(f):
                if f is None:
                    return
                act.wait_ge(var1_ready, done(f, 1, 1))
                if not first(f, 1):
                    act.wait_ge(h1_ready, done(f, 1, 0))
                act.activation(rstd1[:, :], FB, ACT.Ln, bias=eps[:, :]).then_inc(log1, 1)

            def exp_var1(f):
                if f is None:
                    return
                act.wait_ge(log1, done(f, 1, 1))
                act.activation(rstd1[:, :], rstd1[:, :], ACT.Exp, scale=-0.5).then_inc(rstd1_ready, 1)

            def log_var2(p):
                if p is None:
                    return
                act.wait_ge(var2_ready, done(p, 1, 1))
                if not first(p, 1):
                    act.wait_ge(h2_ready, done(p, 1, 0))
                act.activation(rstd2[:, :], banks(p)[0], ACT.Ln, bias=eps[:, :]).then_inc(log2, 1)

            def exp_var2(p):
                if p is None:
                    return
                act.wait_ge(log2, done(p, 1, 1))
                act.activation(rstd2[:, :], rstd2[:, :], ACT.Exp, scale=-0.5).then_inc(rstd2_ready, 1)

            def step(f, a, s, b, p):
                first_part(a, 0)
                exp_tile(b, 6)
                first_part(a, 1)
                copy_bank(b, 0)
                copy_bank(b, 1)
                exp_tile(b, 7)
                log_den(p, 1)
                exp_den(p, 1)
                copy_bank(b, 2)
                copy_bank(b, 3)
                square1(f)
                copy_v(s)
                exp_tile(s, 0)
                copy_bank(b, 4)
                exp_tile(s, 1)
                square2(p)
                exp_tile(s, 2)
                log_var1(f)
                copy_bank(b, 5)
                log_var2(p)
                exp_var2(p)
                exp_var1(f)
                exp_tile(s, 3)
                exp_tile(s, 4)
                copy_bank(b, 6)
                log_den(b, 0)
                exp_den(b, 0)
                copy_bank(b, 7)
                exp_tile(s, 5)

            act.wait_ge(const_ready, 1)
            steps(act, step, {0: lambda: act.wait_ge(weights_ready, 1)})
            p, b = before_last, last
            copy_bank(b, 0)
            exp_tile(b, 6)
            copy_bank(b, 1)
            exp_tile(b, 7)
            log_den(p, 1)
            copy_bank(b, 2)
            exp_den(p, 1)
            copy_bank(b, 3)
            square2(p)
            copy_bank(b, 4)
            copy_bank(b, 5)
            log_den(b, 0)
            copy_bank(b, 6)
            exp_den(b, 0)
            log_var2(p)
            copy_bank(b, 7)
            exp_var2(p)
            log_den(b, 1)
            exp_den(b, 1)

            def gelu(i2, u):
                for g in range(G):
                    act.wait_ge(hidden_ready, (i2 * 2 + u) * G + g + 1)
                    if not (isinstance(i2, int) and i2 == 0):
                        act.wait_ge(down_ready, (i2 * 2 + (u - 1)) * G + (g + 1 - G))
                    act.activation(hid[:, u, g, :], ps[:, g, :], ACT.Gelu, bias=fb1[:, :]).then_inc(gelu_ready, 1)

            gelu(0, 0)
            square2(last)
            gelu(0, 1)
            log_var2(last)
            exp_var2(last)
            act.preload_act_table_set("gelu_and_others")
            with act.Fori(1, NCH // 2) as i2:
                gelu(i2, 0)
                gelu(i2, 1)

        @block.vector
        def _(dve):
            n_setup = [0]

            def link(ins):
                n_setup[0] += 1
                ins.then_inc(setup_v, 1)
                dve.wait_ge(setup_v, n_setup[0])

            dve.memset(eps[:, :], 1e-5)
            dve.memset(ones_v[:, :], 0.0)
            link(dve.memset(mean_m[:, :], 0.0))
            for g in range(G):
                dve.memset(mean_m[C * g:C * (g + 1), C * g:C * (g + 1)], 1.0 / C)
            for v in range(2):
                ins = dve.memset(ones_v[64 * v:64 * (v + 1), HC * v:HC * (v + 1)], 1.0)
            link(ins)
            dve.wait_ge(ident_ready, 2)
            dve.tensor_tensor(cent_m[:, :], ident[:, :], mean_m[:, :], ALU.subtract).then_inc(const_ready, 1)
            dve.memset(v_blk[:, :, :, :, :], 0.0).then_inc(blank_v, 1)
            dve.memset(q_st[0:KR, 1, :, :, :].rearrange("p g h n -> p (g h n)").bitcast(fp32), 0.0).then_inc(cleared[1], 1)

            def set_up_qkv():
                dve.wait_ge(setup_t, 1)
                dve.wait_ge(blank, 1)
                dve.tensor_copy(vec[:, 0:5], ps[:, 0, 0:5])
                for g in range(G):
                    r = slice(C * g, C * (g + 1))
                    ins = dve.tensor_copy(raw_t[r, 0:3, r], ps[r, 1, 0:3 * C].rearrange("p (s o) -> p s o", s=3))
                link(ins)
                dve.tensor_scalar(wqk[:, 0, :], raw_t[:, 0, :], vec[:, 0:1], HD ** -0.5, ALU.mult, ALU.mult)
                dve.tensor_scalar(wqk[:, 1, :], raw_t[:, 1, :], vec[:, 0:1], None, ALU.mult).then_inc(setup_b, 1)
                dve.tensor_scalar(wv[:, :, :, :].rearrange("p v x e -> p x v e"),
                                  raw_t[:, 2, :].rearrange("p (x v e) -> p x v e", x=2, v=2), vec[:, 0:1], None,
                                  ALU.mult)
                dve.wait_ge(setup_t, 2)
                dve.tensor_scalar(bq[:, 0:1], ps[:, 7, 0:1], vec[:, 2:3], HD ** -0.5, ALU.add, ALU.mult)
                dve.tensor_scalar(bq[:, 1:2], ps[:, 7, 1:2], vec[:, 3:4], None, ALU.add)
                dve.tensor_scalar(bq[:, 2:3], ps[:, 7, 2:3], vec[:, 4:5], None, ALU.add).then_inc(weights_ready, 1)
                dve.wait_ge(weights_ready, 1)
                dve.wait_ge(late_in, 16 * 8)
                dve.wait_ge(blank, 2)
                for a in range(2):
                    for v in range(2):
                        r = slice(C * (2 * a + v), C * (2 * a + v + 1))
                        dve.tensor_copy(nat[r, 0, r], p_nat[r, :])
                        for hh in range(2):
                            dst = nat[r, 1 + hh, :].rearrange("p (x q v e) -> p x q v e", x=2, q=2, v=2)
                            src = p_nat[r, :].rearrange("p (q e) -> p q e", q=2)
                            ins = dve.tensor_copy(dst[:, a, :, v, HD * hh:HD * (hh + 1)],
                                                  src[:, :, HD * hh:HD * (hh + 1)])
                ins.then_inc(nat_ready, 1)

            def set_up_copies():
                dve.wait_ge(setup_t, 3)
                dve.tensor_copy(vec[:, 5:9], ps[:, 7, 16 + 5:16 + 9])
                dve.tensor_copy(raw_t[:, 3, :], ps[:, 2, 0:128])
                dve.tensor_copy(f1_t[:, :], ps[:, 3, 0:HID])
                dve.tensor_copy(wp[:, :, :], ps[:, 2, 128:384].rearrange("p (h o) -> p h o", h=2))
                dve.tensor_copy(f2_st[:, :], ps[:, 3, HID:HID + C]).then_inc(setup_b, 1)
                dve.wait_ge(setup_b, 2)

            def set_up_rest():
                link(dve.tensor_scalar(f1_s[:, 0, :], f1_t[:, :], vec[:, 6:7], None, ALU.mult))
                link(dve.tensor_copy(f1_p[:, 0, :], f1_s[:, 0, :]))
                link(dve.tensor_tensor(f1_s[:, 1, :], f1_s[:, 0, :], f1_p[:, 0, :], ALU.subtract))
                link(dve.tensor_copy(f1_p[:, 1, :], f1_s[:, 1, :]))
                link(dve.tensor_tensor(f1_p[:, 2, :], f1_s[:, 1, :], f1_p[:, 1, :], ALU.subtract))
                for i, row, end, part in ((0, 0, 2, 0), (0, 2, 3, 0), (0, 3, 4, 1), (1, 0, 1, 2), (1, 1, 2, 1)):
                    dve.tensor_copy(f1_st[C * row:C * end, i, :], f1_p[C * row:C * end, part, :])
                dve.wait_ge(setup_t, 4)
                dve.tensor_scalar(fb1[:, :], ps[:, 7, 3:4], fc1_bc[:, :], None, ALU.add)
                dve.tensor_scalar(bq[:, 3:4], ps[:, 6, 0:1], vec[:, 5:6], None, ALU.add).then_inc(weights_ready, 1)
                dve.wait_ge(weights_ready, 2)

            def make_table():
                dve.wait_ge(bias_in, 16 * WS)
                table = raw_b[:, :, :].rearrange("p y (x h) -> p y x h", h=NH)
                for hh in range(2):
                    for pr in range(2):
                        ins = dve.tensor_copy(bias_t[NT * hh:NT * (hh + 1), pr, :, :], table[:, ::-1, ::-1, 2 * pr + hh])
                ins.then_inc(table_ready, 1)
                dve.wait_ge(table_ready, 1)

            bias_pair = bias_t[:, :, :, :].rearrange("p q y x -> p q (y x)")

            def divide(c, half):
                if c is None:
                    return
                dve.wait_ge(attended, done(c, 2, half + 1))
                dve.wait_ge(den_ready, done(c, 2, half + 1))
                if half == 0 and not first(c, 1):
                    dve.wait_ge(projected, done(c, 1, 0))
                for hh in range(2):
                    dst = att[:, hh, :].rearrange("p (i w j) -> p w i j", i=WS, j=WS)[:, 4 * half:4 * half + 4]
                    src = banks(c)[0].rearrange("p (w h i j) -> p h w i j", w=4, h=2, i=WS)[:, hh]
                    ins = dve.tensor_tensor(dst, src, den[:, :, hh, :].rearrange("p w (i j) -> p w i j", i=WS),
                                            ALU.mult)
                ins.then_inc(divided, 1)

            def rest_of(a, i):
                if a is None:
                    return
                dve.wait_ge((q_ready, k_ready)[i], done(a, 1, 1))
                dve.wait_ge(part0, done(a, 2, i + 1))
                if not first(a, 1):
                    dve.wait_ge(part2, done(a, 2, i + 1) - 2)
                dve.scalar_tensor_tensor(out=rest[:, i, :], in0=(FA, FB)[i], scalar=bq[:, i:i + 1],
                                         in1=parts[:, a[1], i, 0, :], op0=ALU.add, op1=ALU.subtract)\
                   .then_inc(resid, 1)

            def second_part(a, i):
                if a is None:
                    return
                dve.wait_ge(resid, done(a, 2, i + 1))
                if not first(a, 2):
                    dve.wait_ge(parts_out[a[1]][i], a[0] * 48)
                dve.tensor_copy(parts[:, a[1], i, 1, :], rest[:, i, :]).then_inc(part1, 1)

            def add_bias(s, k):
                if s is None:
                    return
                if first(s, 1) and k == 0:
                    make_table()
                dve.wait_ge(scores_ready, done(s, GP, k + 1))
                if k == 0 and not first(s, 2):
                    dve.wait_ge(transposed, done(s, 8, 0) - 8)
                pair = (k // 2) % 2
                dve.tensor_tensor(prob[:, s[1], k // 2, :, k % 2, :], S_PS[k % 2].rearrange("p (w m) -> p w m", m=NT),
                                  bias_pair[:, pair, :].unsqueeze(1).to_broadcast([128, NW, NT]),
                                  ALU.add).then_inc(biased, 1)

            def find_max(s, k):
                if s is None:
                    return
                dve.wait_ge(biased, done(s, GP, k + 1))
                if not (first(s, 1) and k < 2):
                    dve.wait_ge(shifted, done(s, GP, k + 1) - 2)
                dve.reduce_max(mx[:, k % 2, :], prob[:, s[1], k // 2, :, k % 2, :], AX.X).then_inc(maxed, 1)

            def residual(p):
                if p is None:
                    return
                dve.wait_ge(projected, done(p, 1, 1))
                dve.scalar_tensor_tensor(out=cols(x1_sb, p), in0=banks(p)[0], scalar=bq[:, 3:4],
                                         in1=cols(x_sb, p), op0=ALU.add, op1=ALU.add).then_inc(x1_ready, 1)

            def norm2(p):
                if p is None:
                    return
                dve.wait_ge(rstd2_ready, done(p, 1, 1))
                if not first(p, 1):
                    dve.wait_ge(h2_part2, done(p, 1, 0))
                dve.tensor_tensor(h2[:, :], banks(p)[1], rstd2[:, :], ALU.mult).then_inc(h2_ready, 1)

            def norm1(f):
                if f is None:
                    return
                dve.wait_ge(rstd1_ready, done(f, 1, 1))
                if not first(f, 2):
                    dve.wait_ge(v_ready, done(f, 1, 0) - 1)
                dve.tensor_tensor(h1[:, f[1], :, :].rearrange("p w (i j) -> p w i j", i=WS),
                                  FA.rearrange("p (i w j) -> p w i j", i=WS, j=WS),
                                  rstd1[:, :].rearrange("p (i w j) -> p w i j", i=WS, j=WS),
                                  ALU.mult).then_inc(h1_ready, 1)

            def first_h2(p):
                if p is None:
                    return
                dve.wait_ge(h2_ready, done(p, 1, 1))
                if not first(p, 1):
                    dve.wait_ge(h2_out, done(p, 48, 0))
                dve.tensor_copy(h2_p[:, 0, :], h2[:, :]).then_inc(h2_part0, 1)

            def second_h2(p):
                if p is None:
                    return
                dve.wait_ge(h2_rest, done(p, 1, 1))
                dve.tensor_copy(h2_p[:, 1, :], h2[:, :]).then_inc(h2_part1, 1)

            def step(f, a, s, b, p):
                rest_of(a, 0)
                second_part(a, 0)
                rest_of(a, 1)
                add_bias(s, 0)
                second_part(a, 1)
                add_bias(s, 1)
                find_max(s, 0)
                divide(p, 1)
                find_max(s, 1)
                add_bias(s, 2)
                add_bias(s, 3)
                residual(p)
                find_max(s, 2)
                add_bias(s, 4)
                find_max(s, 3)
                add_bias(s, 5)
                find_max(s, 4)
                find_max(s, 5)
                add_bias(s, 6)
                norm2(p)
                norm1(f)
                first_h2(p)
                add_bias(s, 7)
                find_max(s, 6)
                divide(b, 0)
                find_max(s, 7)
                second_h2(p)

            steps(dve, step, {0: set_up_qkv, 1: set_up_copies, 2: set_up_rest})
            p, b = before_last, last
            divide(p, 1)
            residual(p)
            divide(b, 0)
            norm2(p)
            first_h2(p)
            divide(b, 1)
            second_h2(p)

            def finish(i2, u):
                dve.wait_ge(down_ready, (i2 * 2 + u) * G + G)
                if not (isinstance(i2, int) and i2 == 0):
                    dve.wait_ge(stored[u], i2 * (16 * 2))
                dve.scalar_tensor_tensor(out=y_sb[:, u, :], in0=OD_PS[u], scalar=vec[:, 8:9],
                                         in1=cols(x1_sb, (i2, u)), op0=ALU.add, op1=ALU.add).then_inc(y_ready, 1)

            residual(last)
            finish(0, 0)
            norm2(last)
            first_h2(last)
            second_h2(last)
            finish(0, 1)
            with dve.Fori(1, NCH // 2) as i2:
                finish(i2, 0)
                finish(i2, 1)

        @block.tensor
        def _(pe):
            def set_up_qkv():
                pe.wait_ge(w_in, 16 * 4)
                pe.transpose(ps[:, 0, 0:5], vec_r[0:5, :, :].rearrange("p g c -> p (g c)"), ident[0:5, 0:5])
                pe.transpose(ps[:, 1, 0:3 * C], w_rep[:, :, :].rearrange("p g c -> p (g c)"), ident[0:3 * C, 0:3 * C])\
                  .then_inc(setup_t, 1)
                pe.wait_ge(setup_b, 1)
                for i in range(3):
                    ins = pe.matmul(ps[:, 7, i:i + 1], raw_t[:, i, :], vec[:, 1:2], start=True, stop=True)
                ins.then_inc(setup_t, 1)

            def set_up_copies():
                pe.wait_ge(late_in, 16 * 8)
                pe.transpose(ps[:, 7, 16:25], vec_r[:, :, :].rearrange("p g c -> p (g c)"), ident[0:9, 0:9])
                pe.transpose(ps[:, 3, 0:HID], f1_rep[:, :, :].rearrange("p g c -> p (g c)"), ident[:, :])
                pe.transpose(ps[:, 3, HID:HID + C], f2_nat[:, :], ident[0:C, 0:C])
                pe.wait_ge(nat_ready, 1)
                for i in range(3):
                    ins = pe.transpose(ps[:, 2, 128 * i:128 * (i + 1)], nat[:, i, :], ident[:, :])
                ins.then_inc(setup_t, 1)

            def set_up_rest():
                pe.wait_ge(setup_b, 2)
                pe.wait_ge(weights_ready, 1)
                pe.matmul(ps[:, 7, 3:4], f1_t[0:C, :], vec[0:C, 7:8], start=True, stop=True)
                pe.matmul(ps[:, 6, 0:1], raw_t[:, 3, :], bq[:, 2:3], start=True, stop=True).then_inc(setup_t, 1)

            def attend(c, half):
                if c is None:
                    return
                pe.wait_ge(prob_copied, done(c, 8, 4 * half + 4))
                pe.wait_ge(v_copied, done(c, 1, 1))
                if half == 1:
                    pe.wait_ge(divided, done(c, 2, 1))
                elif not first(c, 1) and c is not last:
                    pe.wait_ge(log2, done(c, 1, 0))
                for w in range(4):
                    for q in range(XP):
                        ins = pe.matmul(banks(c)[0][32 * q:32 * (q + 1), 128 * w:128 * (w + 1)],
                                        v_blk[:, c[1], 4 * half + w, q, :], prob_t[:, half, q, w, :],
                                        start=True, stop=True, tile_position=(0, 32 * q))
                ins.then_inc(attended, 1)

            def sum_keys(c, half):
                if c is None:
                    return
                if half == 0 and not first(c, 1) and c is not last:
                    pe.wait_ge(h2_ready, done(c, 1, 0))
                if half == 1:
                    pe.wait_ge(den_log, done(c, 2, 1))
                for q in range(XP):
                    ins = pe.matmul(banks(c)[1][32 * q:32 * (q + 1), :], ones_v[:, :],
                                    prob_t[:, half, q, :, :].rearrange("p w n -> p (w n)"),
                                    start=True, stop=True, tile_position=(0, 32 * q))
                ins.then_inc(summed, 1)

            def make_qk(a):
                if a is None:
                    return
                pe.wait_ge(h1_ready, done(a, 1, 1))
                pe.matmul(FA, wqk[:, 0, :], h1[:, a[1], :, :].rearrange("p w n -> p n w"),
                          start=True, stop=True).then_inc(q_ready, 1)
                pe.matmul(FB, wqk[:, 1, :], h1[:, a[1], :, :].rearrange("p w n -> p (w n)"),
                          start=True, stop=True).then_inc(k_ready, 1)

            def score(s, k):
                if s is None:
                    return
                gp = (2 * (k // 4) + k % 2) * 2 + (k // 2) % 2
                if k == 0:
                    pe.wait_ge(stacks_in[s[1]], s[0] * (16 * READS) + 16 * READS)
                if not (first(s, 1) and k < 2):
                    pe.wait_ge(biased, done(s, GP, k + 1) - 2)
                q_w = q_st[0:KR, s[1], gp, :, :].rearrange("p h n -> p (h n)").rearrange("p (m w) -> p w m", w=NW)
                for w in range(NW):
                    ins = pe.matmul(S_PS[k % 2][:, NT * w:NT * (w + 1)], q_w[:, w, :],
                                    k_st[:, s[1], gp, NT * w:NT * (w + 1)], start=True, stop=True)
                ins.then_inc(scores_ready, 1)

            def turn(b, k):
                if b is None:
                    return
                half, q = k // 4, k % 4
                if half == 0:
                    pe.wait_ge(expd, done(b, GP, 2 * q + 2))
                if not (first(b, 1) and k < 2):
                    pe.wait_ge(prob_copied, done(b, 8, k + 1) - 2)
                for w in range(4):
                    ins = pe.transpose(T_PS[k % 2][:, 128 * w:128 * (w + 1)],
                                       prob[:, b[1], q, 4 * half + w, :, :].rearrange("p v m -> p (v m)"),
                                       ident[:, :])
                ins.then_inc(transposed, 1)

            def project(p):
                if p is None:
                    return
                pe.wait_ge(divided, done(p, 2, 2))
                for hh in range(2):
                    ins = pe.matmul(banks(p)[0], wp[:, hh, :], att[:, hh, :], start=(hh == 0), stop=(hh == 1))
                ins.then_inc(projected, 1)

            def center1(f, a):
                if f is None:
                    return
                for t, (i, loads) in enumerate(((0, 2), (1, 2), (2, G), (3, G))):
                    if first(f, t + 1) and not first(f, t):
                        pe.wait_ge(x_in[i], 16 * loads)
                if a is not None:
                    pe.wait_ge(resid, done(a, 2, 1))
                pe.matmul(FA, cent_m[:, :], cols(x_sb, f), start=True, stop=True).then_inc(centered1, 1)

            def make_v(s, a):
                if s is None:
                    return
                if a is not None:
                    pe.wait_ge(resid, done(a, 2, 2))
                else:
                    pe.wait_ge(v_copied, done(s, 1, 0))
                for w in range(0, NW, 2):
                    ins = pe.matmul(FB[:, NT * w:NT * (w + 2)],
                                    h1[:, s[1], w:w + 2, :].rearrange("p w n -> p (w n)"),
                                    wv[:, :, :, :].rearrange("p v x e -> p (v x e)"), start=True, stop=True)
                ins.then_inc(v_ready, 1)

            def variance1(f, a, s):
                if f is None:
                    return
                pe.wait_ge(squared1, done(f, 1, 1))
                if s is not None:
                    pe.wait_ge(v_copied, done(s, 1, 1))
                elif a is not None:
                    pe.wait_ge(resid, done(a, 2, 2))
                pe.matmul(FB, mean_m[:, :], sq1[:, :], start=True, stop=True).then_inc(var1_ready, 1)

            def center2(p):
                if p is None:
                    return
                pe.wait_ge(x1_ready, done(p, 1, 1))
                pe.matmul(banks(p)[1], cent_m[:, :], cols(x1_sb, p), start=True, stop=True).then_inc(centered2, 1)

            def variance2(p):
                if p is None:
                    return
                pe.wait_ge(squared2, done(p, 1, 1))
                pe.matmul(banks(p)[0], mean_m[:, :], sq2[:, :], start=True, stop=True).then_inc(var2_ready, 1)

            def step(f, a, s, b, p):
                make_qk(a)
                turn(b, 0)
                turn(b, 1)
                attend(p, 1)
                score(s, 0)
                sum_keys(p, 1)
                score(s, 1)
                turn(b, 2)
                turn(b, 3)
                center1(f, a)
                score(s, 2)
                score(s, 3)
                make_v(s, a)
                project(p)
                score(s, 4)
                turn(b, 4)
                score(s, 5)
                center2(p)
                variance1(f, a, s)
                turn(b, 5)
                variance2(p)
                turn(b, 6)
                score(s, 6)
                score(s, 7)
                attend(b, 0)
                sum_keys(b, 0)
                turn(b, 7)

            pe.wait_ge(const_ready, 1)
            steps(pe, step, {0: set_up_qkv, 1: set_up_copies, 2: set_up_rest})
            p, b = before_last, last
            turn(b, 0)
            turn(b, 1)
            attend(p, 1)
            sum_keys(p, 1)
            turn(b, 2)
            turn(b, 3)
            turn(b, 4)
            turn(b, 5)
            project(p)
            attend(b, 0)
            center2(p)
            sum_keys(b, 0)
            turn(b, 6)
            variance2(p)
            turn(b, 7)
            attend(b, 1)
            sum_keys(b, 1)

            pe.wait_ge(prob_copied, 8 * NCH)
            pe.wait_ge(weights_ready, 2)
            pe.wait_ge(h2_in[0], 32 * (NCH - 2))

            def up(i2, u, g):
                if not (isinstance(i2, int) and 2 * i2 + u == 0):
                    pe.wait_ge(gelu_ready, (i2 * 2 + u) * G + (g + 1 - G))
                if isinstance(i2, int):
                    rows = h2_st[:, 2 * i2 + u, g, :]
                else:
                    rows = h2_st.rearrange("p (i u) g n -> p i u g n", u=2)[:, bass.ds(i2, 1), u, g, :]\
                        .rearrange("p o n -> p (o n)")
                for i in range(2):
                    ins = pe.matmul(ps[:, g, :], f1_st[:, i, :], rows, start=(i == 0), stop=(i == 1))
                ins.then_inc(hidden_ready, 1)

            def down(i2, u, g):
                if g == 0 and not (isinstance(i2, int) and i2 == 0):
                    pe.wait_ge(y_ready, i2 * 2 + (u - 1))
                pe.wait_ge(gelu_ready, (i2 * 2 + u) * G + g + 1)
                pe.matmul(OD_PS[u][C * g:C * (g + 1), :], f2_st[:, :], hid[:, u, g, :], start=True, stop=True,
                          tile_position=(0, C * g)).then_inc(down_ready, 1)

            for g in range(G):
                up(0, 0, g)
            project(last)
            for g in range(G):
                if g == 2:
                    center2(last)
                up(0, 1, g)
                down(0, 0, g)
            variance2(last)
            with pe.Fori(1, NCH // 2 - 1) as i2:
                for g in range(G):
                    up(i2, 0, g)
                    down(i2 - 1, 1, g)
                for g in range(G):
                    up(i2, 1, g)
                    down(i2, 0, g)
            pe.wait_ge(h2_in[1], 32)
            for g in range(G):
                up(NCH // 2 - 1, 0, g)
                down(NCH // 2 - 2, 1, g)
            pe.wait_ge(h2_in[2], 32)
            for g in range(G):
                up(NCH // 2 - 1, 1, g)
                down(NCH // 2 - 1, 0, g)
            for g in range(G):
                down(NCH // 2 - 1, 1, g)


_INS = ['x', 'L0_conv_ln1_g', 'L0_conv_ln1_b', 'L0_conv_qkv_w', 'L0_conv_qkv_b', 'L0_conv_rpb', 'L0_conv_proj_w',
        'L0_conv_proj_b', 'L0_conv_ln2_g', 'L0_conv_ln2_b', 'L0_conv_fc1_w', 'L0_conv_fc1_b', 'L0_conv_fc2_w',
        'L0_conv_fc2_b']


def kernel(**inputs):
    import numpy as _np
    import concourse.bacc as _bacc
    from concourse import mybir as _mybir
    from concourse.bass_utils import run_bass_kernel_spmd as _run

    nc = _bacc.Bacc("TRN2", target_bir_lowering=False, num_devices=1)
    arrays, args = {}, []
    for name in _INS:
        a = _np.ascontiguousarray(inputs[name])
        arrays[f"in_{name}_dram"] = a
        args.append(nc.dram_tensor(f"in_{name}_dram", a.shape, _mybir.dt.from_np(a.dtype), kind="ExternalInput").ap())
    shape = _np.shape(inputs['x'])
    args.append(nc.dram_tensor("out_0_dram", shape, _mybir.dt.float32, kind="ExternalOutput").ap())
    swin_block_kernel(nc, *args)
    r = _run(nc, [arrays], core_ids=[0])
    return r.results[0]["out_0_dram"]
```
